# Optimizing a Trainium2 kernel written in Bass

```python
import numpy as np
import jax
import jax.numpy as jnp

def _softmax(x, axis=-1):
    return jax.nn.softmax(x, axis=axis)

def _gelu(x):
    return jax.nn.gelu(x, approximate=True)

def _silu(x):
    return jax.nn.silu(x)

def _sigmoid(x):
    return jax.nn.sigmoid(x)

def _layernorm(x, axis=-1, eps=1e-05):
    m = jnp.mean(x, axis=axis, keepdims=True)
    v = jnp.var(x, axis=axis, keepdims=True)
    return (x - m) / jnp.sqrt(v + eps)

def _scatter_add(tgt, idx, src, axis=0):
    return tgt.at[idx].add(src)

def _segment_sum(src, seg, n):
    return jax.ops.segment_sum(src, seg, n)
kernel_name = 'mk_early_fusion_d1_tok_img512_r4_0fade8'

def setup_inputs(seed: int=0):
    np.random.seed(seed)
    _w = jnp.asarray

    def _rec_inputs():
        import jax
        import jax.numpy as jnp
        _rk = jax.random.key(seed)
        x = 7.57192e-06 + 1.00007 * jax.random.normal(jax.random.fold_in(_rk, 1), (64, 3, 224, 224), jnp.float32)
        txt = -1.28643e-11 + 0.999988 * jax.random.normal(jax.random.fold_in(_rk, 2), (64, 77, 128), jnp.float32)
        return (x, txt)
    x, txt = _rec_inputs()

    def _L0_tok_setup():
        import jax, jax.numpy as jnp
        import numpy as np
        DEPTH = 4
        HEADS = 8
        DIM = 128
        HID = 256
        P = 16
        IMG = 224
        GRID = IMG // P
        NPATCH = GRID * GRID
        NTOK = NPATCH + 1
        BATCH = 64
        EPS = 1e-05

        def layernorm(x, w, b):
            mu = jnp.mean(x, axis=-1, keepdims=True)
            var = jnp.mean(jnp.square(x - mu), axis=-1, keepdims=True)
            return (x - mu) * jax.lax.rsqrt(var + EPS) * w + b
        key = jax.random.key(seed)
        ks = jax.random.split(key, 12)
        s = 0.02
        inp = {'x': jax.random.normal(ks[0], (BATCH, 3, IMG, IMG), jnp.float32), 'conv_w': jax.random.normal(ks[1], (3 * P * P, DIM), jnp.float32) * s, 'conv_b': jnp.zeros((DIM,), jnp.float32), 'cls_token': jax.random.normal(ks[2], (1, 1, DIM), jnp.float32) * s, 'pos_embed': jax.random.normal(ks[3], (1, NTOK, DIM), jnp.float32) * s, 'ln1_w': jnp.ones((DEPTH, DIM), jnp.float32), 'ln1_b': jnp.zeros((DEPTH, DIM), jnp.float32), 'qkv_w': jax.random.normal(ks[4], (DEPTH, DIM, 3 * DIM), jnp.float32) * s, 'qkv_b': jnp.zeros((DEPTH, 3 * DIM), jnp.float32), 'proj_w': jax.random.normal(ks[5], (DEPTH, DIM, DIM), jnp.float32) * s, 'proj_b': jnp.zeros((DEPTH, DIM), jnp.float32), 'ln2_w': jnp.ones((DEPTH, DIM), jnp.float32), 'ln2_b': jnp.zeros((DEPTH, DIM), jnp.float32), 'fc1_w': jax.random.normal(ks[6], (DEPTH, DIM, HID), jnp.float32) * s, 'fc1_b': jnp.zeros((DEPTH, HID), jnp.float32), 'fc2_w': jax.random.normal(ks[7], (DEPTH, HID, DIM), jnp.float32) * s, 'fc2_b': jnp.zeros((DEPTH, DIM), jnp.float32), 'norm_w': jnp.ones((DIM,), jnp.float32), 'norm_b': jnp.zeros((DIM,), jnp.float32)}
        return inp
    _L0_tok_all = _L0_tok_setup()
    _L0_tok_in = {k: v for k, v in _L0_tok_all.items() if k in ('conv_w', 'conv_b', 'cls_token', 'pos_embed', 'ln1_w', 'ln1_b', 'qkv_w', 'qkv_b', 'proj_w', 'proj_b', 'ln2_w', 'ln2_b', 'fc1_w', 'fc1_b', 'fc2_w', 'fc2_b', 'norm_w', 'norm_b')}
    del _L0_tok_all

    def _L0_attn_setup():
        import jax, jax.numpy as jnp
        import numpy as np
        NUM_HEADS = 8
        key = jax.random.key(seed)
        k1, k2, k3 = jax.random.split(key, 3)
        B, N, C = (4, 512, 128)
        x = jax.random.normal(k1, (B, N, C), dtype=jnp.float32)
        q_w = jax.random.normal(k2, (C, C), dtype=jnp.float32) * 0.02
        kv_w = jax.random.normal(k3, (2 * C, C), dtype=jnp.float32) * 0.02
        return {'x': x, 'q_w': q_w, 'kv_w': kv_w}
    _L0_attn_all = _L0_attn_setup()
    _L0_attn_in = {k: v for k, v in _L0_attn_all.items() if k in ('q_w', 'kv_w')}
    del _L0_attn_all

    def _L0_ffn_setup():
        import jax, jax.numpy as jnp
        import numpy as np
        D = 128
        E = 8
        K = 2
        EXP = 4
        LN_EPS = 1e-05
        key = jax.random.key(seed)
        ks = jax.random.split(key, 8)
        B, T = (8, 512)
        Dh = D * EXP
        x = jax.random.normal(ks[0], (B, T, D), dtype=jnp.float32)
        ln_g = jnp.ones((D,), dtype=jnp.float32)
        ln_b = jnp.zeros((D,), dtype=jnp.float32)
        lim_r = np.sqrt(6.0 / (D + E)).astype(np.float32)
        w_r = jax.random.uniform(ks[1], (E, D), dtype=jnp.float32, minval=-lim_r, maxval=lim_r)
        b_r = jnp.zeros((E,), dtype=jnp.float32)
        lim1 = np.sqrt(6.0 / (D + Dh)).astype(np.float32)
        W1 = jax.random.uniform(ks[2], (E, D, Dh), dtype=jnp.float32, minval=-lim1, maxval=lim1)
        b1 = jnp.zeros((E, Dh), dtype=jnp.float32)
        W2 = jax.random.uniform(ks[3], (E, Dh, D), dtype=jnp.float32, minval=-lim1, maxval=lim1)
        b2 = jnp.zeros((E, D), dtype=jnp.float32)
        return {'x': x, 'ln_g': ln_g, 'ln_b': ln_b, 'w_r': w_r, 'b_r': b_r, 'W1': W1, 'b1': b1, 'W2': W2, 'b2': b2}
    _L0_ffn_all = _L0_ffn_setup()
    _L0_ffn_in = {k: v for k, v in _L0_ffn_all.items() if k in ('ln_g', 'ln_b', 'w_r', 'b_r', 'W1', 'b1', 'W2', 'b2')}
    del _L0_ffn_all
    return {'x': x, 'txt': txt, 'L0_tok_conv_w': _L0_tok_in['conv_w'], 'L0_tok_conv_b': _L0_tok_in['conv_b'], 'L0_tok_cls_token': _L0_tok_in['cls_token'], 'L0_tok_pos_embed': _L0_tok_in['pos_embed'], 'L0_tok_ln1_w': _L0_tok_in['ln1_w'], 'L0_tok_ln1_b': _L0_tok_in['ln1_b'], 'L0_tok_qkv_w': _L0_tok_in['qkv_w'], 'L0_tok_qkv_b': _L0_tok_in['qkv_b'], 'L0_tok_proj_w': _L0_tok_in['proj_w'], 'L0_tok_proj_b': _L0_tok_in['proj_b'], 'L0_tok_ln2_w': _L0_tok_in['ln2_w'], 'L0_tok_ln2_b': _L0_tok_in['ln2_b'], 'L0_tok_fc1_w': _L0_tok_in['fc1_w'], 'L0_tok_fc1_b': _L0_tok_in['fc1_b'], 'L0_tok_fc2_w': _L0_tok_in['fc2_w'], 'L0_tok_fc2_b': _L0_tok_in['fc2_b'], 'L0_tok_norm_w': _L0_tok_in['norm_w'], 'L0_tok_norm_b': _L0_tok_in['norm_b'], 'L0_attn_q_w': _L0_attn_in['q_w'], 'L0_attn_kv_w': _L0_attn_in['kv_w'], 'L0_ffn_ln_g': _L0_ffn_in['ln_g'], 'L0_ffn_ln_b': _L0_ffn_in['ln_b'], 'L0_ffn_w_r': _L0_ffn_in['w_r'], 'L0_ffn_b_r': _L0_ffn_in['b_r'], 'L0_ffn_W1': _L0_ffn_in['W1'], 'L0_ffn_b1': _L0_ffn_in['b1'], 'L0_ffn_W2': _L0_ffn_in['W2'], 'L0_ffn_b2': _L0_ffn_in['b2']}

def reference(x, txt, L0_tok_conv_w, L0_tok_conv_b, L0_tok_cls_token, L0_tok_pos_embed, L0_tok_ln1_w, L0_tok_ln1_b, L0_tok_qkv_w, L0_tok_qkv_b, L0_tok_proj_w, L0_tok_proj_b, L0_tok_ln2_w, L0_tok_ln2_b, L0_tok_fc1_w, L0_tok_fc1_b, L0_tok_fc2_w, L0_tok_fc2_b, L0_tok_norm_w, L0_tok_norm_b, L0_attn_q_w, L0_attn_kv_w, L0_ffn_ln_g, L0_ffn_ln_b, L0_ffn_w_r, L0_ffn_b_r, L0_ffn_W1, L0_ffn_b1, L0_ffn_W2, L0_ffn_b2):
    import jax
    import jax.numpy as jnp

    def _L0_tok_ref(x, conv_w, conv_b, cls_token, pos_embed, ln1_w, ln1_b, qkv_w, qkv_b, proj_w, proj_b, ln2_w, ln2_b, fc1_w, fc1_b, fc2_w, fc2_b, norm_w, norm_b):
        import jax, jax.numpy as jnp
        import numpy as np
        DEPTH = 4
        HEADS = 8
        DIM = 128
        HID = 256
        P = 16
        IMG = 224
        GRID = IMG // P
        NPATCH = GRID * GRID
        NTOK = NPATCH + 1
        BATCH = 64
        EPS = 1e-05

        def layernorm(x, w, b):
            mu = jnp.mean(x, axis=-1, keepdims=True)
            var = jnp.mean(jnp.square(x - mu), axis=-1, keepdims=True)
            return (x - mu) * jax.lax.rsqrt(var + EPS) * w + b
        B = x.shape[0]
        hd = DIM // HEADS
        scale = hd ** (-0.5)
        patches = x.reshape(B, 3, GRID, P, GRID, P)
        patches = patches.transpose(0, 2, 4, 1, 3, 5).reshape(B, NPATCH, 3 * P * P)
        tok = patches @ conv_w + conv_b
        cls = jnp.broadcast_to(cls_token, (B, 1, DIM))
        h = jnp.concatenate([cls, tok], axis=1) + pos_embed
        for i in range(DEPTH):
            y = layernorm(h, ln1_w[i], ln1_b[i])
            qkv = (y @ qkv_w[i] + qkv_b[i]).reshape(B, NTOK, 3, HEADS, hd)
            qkv = qkv.transpose(2, 0, 3, 1, 4)
            q, k, v = (qkv[0], qkv[1], qkv[2])
            attn = jax.nn.softmax(jnp.einsum('bhnd,bhmd->bhnm', q, k) * scale, axis=-1)
            o = jnp.einsum('bhnm,bhmd->bhnd', attn, v)
            o = o.transpose(0, 2, 1, 3).reshape(B, NTOK, DIM)
            h = h + (o @ proj_w[i] + proj_b[i])
            y = layernorm(h, ln2_w[i], ln2_b[i])
            y = jax.nn.gelu(y @ fc1_w[i] + fc1_b[i], approximate=False)
            h = h + (y @ fc2_w[i] + fc2_b[i])
        return layernorm(h, norm_w, norm_b)

    def _L0_attn_ref(x, q_w, kv_w):
        import jax, jax.numpy as jnp
        import numpy as np
        NUM_HEADS = 8
        B, N, C = x.shape
        H = NUM_HEADS
        D = C // H
        halfB = B // 2
        q = (x @ q_w.T).reshape(B, N, H, D)
        kv = (x @ kv_w.T).reshape(B, N, 2, H, D)
        k, v = (kv[:, :, 0], kv[:, :, 1])
        k = jnp.concatenate([k[halfB:], k[:halfB]], axis=0)
        v = jnp.concatenate([v[halfB:], v[:halfB]], axis=0)
        scores = jnp.einsum('bnhd,bmhd->bhnm', q, k) / jnp.sqrt(jnp.float32(C))
        prob = jax.nn.softmax(scores, axis=-1)
        out = jnp.einsum('bhnm,bmhd->bndh', prob, v).reshape(B, N, C)
        return out

    def _L0_ffn_ref(x, ln_g, ln_b, w_r, b_r, W1, b1, W2, b2):
        import jax, jax.numpy as jnp
        import numpy as np
        D = 128
        E = 8
        K = 2
        EXP = 4
        LN_EPS = 1e-05
        B, T, d = x.shape
        mu = jnp.mean(x, axis=-1, keepdims=True)
        var = jnp.mean(jnp.square(x - mu), axis=-1, keepdims=True)
        h = (x - mu) * jax.lax.rsqrt(var + LN_EPS) * ln_g + ln_b
        logits = jnp.einsum('btd,ed->bte', h, w_r) + b_r
        topk_vals, topk_idx = jax.lax.top_k(logits, K)
        gates = jax.nn.softmax(topk_vals, axis=-1)
        hf = h.reshape(B * T, d)
        hid = jax.nn.gelu(jnp.einsum('nd,edf->nef', hf, W1) + b1, approximate=False)
        expert_stack = jnp.einsum('nef,efd->ned', hid, W2) + b2
        idx_flat = topk_idx.reshape(B * T, K)
        gates_flat = gates.reshape(B * T, K)
        gathered = jnp.take_along_axis(expert_stack, idx_flat[:, :, None], axis=1)
        mixed = jnp.sum(gathered * gates_flat[:, :, None], axis=1).reshape(B, T, d)
        return x + mixed
    h = _L0_tok_ref(x, L0_tok_conv_w, L0_tok_conv_b, L0_tok_cls_token, L0_tok_pos_embed, L0_tok_ln1_w, L0_tok_ln1_b, L0_tok_qkv_w, L0_tok_qkv_b, L0_tok_proj_w, L0_tok_proj_b, L0_tok_ln2_w, L0_tok_ln2_b, L0_tok_fc1_w, L0_tok_fc1_b, L0_tok_fc2_w, L0_tok_fc2_b, L0_tok_norm_w, L0_tok_norm_b)
    h = jnp.concatenate([h, txt], axis=1)
    h = h + _L0_attn_ref(_layernorm(h, axis=-1), L0_attn_q_w, L0_attn_kv_w)
    h = h + _L0_ffn_ref(_layernorm(h, axis=-1), L0_ffn_ln_g, L0_ffn_ln_b, L0_ffn_w_r, L0_ffn_b_r, L0_ffn_W1, L0_ffn_b1, L0_ffn_W2, L0_ffn_b2)
    return h

_drawn_inputs = setup_inputs


def setup_inputs(seed=0):
    import zlib

    import numpy as np

    out = dict(_drawn_inputs(seed))
    spreads = {'L0_tok_conv_b': (0.0, 0.1),
     'L0_tok_ln1_w': (1.0, 0.6),
     'L0_tok_ln1_b': (0.0, 0.41),
     'L0_tok_qkv_b': (0.0, 0.1),
     'L0_tok_proj_b': (0.0, 0.1),
     'L0_tok_ln2_w': (1.0, 0.579),
     'L0_tok_ln2_b': (0.0, 0.528),
     'L0_tok_fc1_b': (0.0, 0.1),
     'L0_tok_fc2_b': (0.0, 0.1),
     'L0_tok_norm_w': (1.0, 0.2),
     'L0_tok_norm_b': (0.0, 0.1),
     'L0_ffn_ln_g': (1.0, 0.2),
     'L0_ffn_ln_b': (0.0, 0.1),
     'L0_ffn_b_r': (0.0, 0.1),
     'L0_ffn_b1': (0.0, 0.273),
     'L0_ffn_b2': (0.0, 0.1)}
    factors = {'L0_tok_cls_token': 8.0, 'L0_attn_q_w': 58.167}
    for name, (base, spread) in spreads.items():
        noise = np.random.default_rng([zlib.crc32(name.encode()), seed]).standard_normal(out[name].shape)
        drawn = base * np.exp(spread * noise) if base else spread * noise
        out[name] = jnp.asarray(drawn.astype(out[name].dtype))
    for name, factor in factors.items():
        out[name] = (out[name] * factor).astype(out[name].dtype)
    return out
```

```python
from contextlib import ExitStack

import concourse.bass as bass
from concourse import mybir

F32 = mybir.dt.float32
BF16 = mybir.dt.bfloat16
ALU = mybir.AluOpType
ACT = mybir.ActivationFunctionType
AX = mybir.AxisListType

P = 128
BATCH = 64
HALF = BATCH // 2
DEPTH = 4
DIM = 128
HEADS = 8
HD = DIM // HEADS
HID = 256
IMG = 224
PATCH = 16
GRID = IMG // PATCH
NPATCH = GRID * GRID
NTOK = NPATCH + 1
TXT = 77
EXPERTS = 8
EHID = 512
EPS = 1e-5
RT = 99
NVIT = 2 * RT
NALL = TXT + NVIT
ROWS = (TXT, RT, RT)
PIX = PATCH // 2
CROWS = 3 * PATCH
SHIFT = 64
GROUP = 32
VBIAS = 9
SLOTS = 4
G_EXP = 19
G_ALL = G_EXP + 6
LEAD = 2


class Step:

    def __init__(self, i, u):
        if u >= SLOTS:
            i, u = i + 1, u - SLOTS
        elif u < 0:
            i, u = i - 1, u + SLOTS
        self.i, self.u = i, u
        self.n = i * SLOTS + u
        self.k = self.n if isinstance(i, int) else None
        self.sample = i * (SLOTS // 2) + (u // 2 + HALF * (u % 2))

    def at(self, d):
        return Step(self.i, self.u + d)


def job_order():
    order = []
    for m in range(LEAD):
        order += [("T", m), ("Q", m), ("K", m), ("V", m)]
    order.append(("M", 0))
    for n in range(BATCH):
        if n + LEAD < BATCH:
            order.append(("T", n + LEAD))
        if n:
            order.append(("E0", n - 1))
        if n + LEAD < BATCH:
            order += [("Q", n + LEAD), ("K", n + LEAD), ("V", n + LEAD)]
        if n:
            order += [("E1", n - 1), ("E2", n - 1)]
        if n + 1 < BATCH:
            order.append(("M", n + 1))
    order += [("E0", BATCH - 1), ("E1", BATCH - 1), ("E2", BATCH - 1)]
    return order


JOBS = {job: at for at, job in enumerate(job_order())}
PER_STEP = 8
PHASE_JOBS = len(JOBS) // 2
INNER = 5


def bank_of(name, s):
    if s.k is not None:
        at = JOBS[(name, s.k)]
        return at % 2, at // 2
    k = INNER + (s.u - INNER) % SLOTS + SLOTS
    at = JOBS[(name, k)]
    return at % 2, s.n * (PER_STEP // 2) + (at // 2 - k * PER_STEP // 2)


class Attention:

    def __init__(self, cross, sem):
        tag = "x_" if cross else "a_"
        self.cross = cross
        self.tiles = ([(0, TXT, TXT, 0), (1, RT, RT, TXT), (2, RT, RT - 1, TXT + RT)] if cross
                      else [(1, RT, RT, 0), (2, RT, RT - 1, RT)])
        self.nq = NALL if cross else NVIT
        self.nk = self.nq - 1
        self.hpu = 1 if cross else 2
        self.upt = HEADS // self.hpu
        self.units = len(self.tiles) * self.upt
        self.slots = ([[] for _ in range(4)] + [[2 * w, 2 * w + 1] for w in range(4)]
                      + [[8 + w] for w in range(16)] if cross else [[w] for w in range(self.units)])
        self.tail = 15 if cross else 4
        self.xn_ready = sem(tag + "xn_ready")
        self.job_done = [sem(tag + f"job_done{i}") for i in range(2)]
        self.job_taken = [sem(tag + f"job_taken{i}") for i in range(2)]
        self.keys_ready = sem(tag + "keys_ready")
        self.qlow_ready = sem(tag + "qlow_ready")
        self.qhead_ready = sem(tag + "qhead_ready")
        self.plain_ready = sem(tag + "plain_ready")
        self.max_taken = sem(tag + "max_taken")
        self.score_ready = sem(tag + "score_ready")
        self.exp_ready = sem(tag + "exp_ready")
        self.pv_done = sem(tag + "pv_done")
        self.out_ready = sem(tag + "out_ready")
        self.link = sem(tag + "link")
        self.bias_added = sem(tag + "bias_added")

    def kv(self, s):
        return s.at(1 if s.u % 2 == 0 else -1) if self.cross else s

    def last_kv(self, s):
        return s.at(1) if self.cross and s.u % 2 == 0 else s


def fusion_kernel(nc, d, out):
    with ExitStack() as ctx:
        def sb(name, shape, dt=F32):
            return ctx.enter_context(nc.sbuf_tensor(name, shape, dt))

        def sem(name):
            return ctx.enter_context(nc.semaphore(name))

        h = sb("h", [P, BATCH * 3 * DIM])
        big = sb("big", [P, 2 * EXPERTS * EHID])
        imgs = [big[:, s * GRID * IMG:(s + 1) * GRID * IMG] for s in range(2)]
        w1 = big[:, 0:EXPERTS * EHID].rearrange("p (e f) -> p e f", e=EXPERTS)
        w2 = big[:, EXPERTS * EHID:2 * EXPERTS * EHID].rearrange("p (e c n) -> p e c n", e=EXPERTS, c=4)
        att = sb("att", [P, 3 * HEADS * NALL])
        NQH = HEADS * NALL
        qhead = [att[:, s * NQH:(s + 1) * NQH] for s in range(2)]
        qlow_all = att[:, 2 * NQH:3 * NQH].bitcast(BF16)
        qlow = [qlow_all[:, s * NQH:(s + 1) * NQH] for s in range(2)]
        wconv = att[:, 0:PIX * DIM].rearrange("p (q n) -> p q n", q=PIX)
        posb = att[:, PIX * DIM:PIX * DIM + 2 * DIM].rearrange("p (t n) -> p t n", t=2)
        eT = att[:, PIX * DIM + 2 * DIM:PIX * DIM + 2 * DIM + 2 * NVIT].rearrange("p (s n) -> p s n", s=2)
        wqkv = sb("wqkv", [P, 3 * DIM])
        wproj = sb("wproj", [P, DIM])
        wfc1 = sb("wfc1", [P, HID])
        wfc2 = sb("wfc2", [P, 2, DIM])
        vec_a = sb("vec_a", [P, 5])
        vec_m = sb("vec_m", [P, 4])
        row_a = sb("row_a", [P, DIM])
        row_m = sb("row_m", [P, DIM])
        row_v = sb("row_v", [P, P])
        qbias = sb("qbias", [P, 1])
        wx = sb("wx", [P, 3 * DIM])
        norm_rows = sb("norm_rows", [P, 2, DIM])
        vec_f = sb("vec_f", [P, 2 + EXPERTS * 4])
        w_r = sb("w_r", [P, EXPERTS])
        b_r = sb("b_r", [P, EXPERTS])
        br2 = sb("br2", [P, 2 * EXPERTS])
        b2 = sb("b2", [P, DIM])
        ident = sb("ident", [P, P])
        identb = sb("identb", [P, P], BF16)
        mask = sb("mask", [P, HEADS])
        rank = sb("rank", [P, EXPERTS])
        sel32 = sb("sel32", [P, HEADS])
        sel = sb("sel", [P, HEADS, RT], BF16)
        eps = sb("eps", [P, 1])
        xn = sb("xn", [P, 2, 3, DIM])
        yT = sb("yT", [P, 2, NALL])
        qt = sb("qt", [P, 2, NALL])
        k32 = sb("k32", [P, SLOTS, NALL])
        klow = sb("klow", [P, SLOTS, NALL + 1], BF16)
        vaug = sb("vaug", [P, SLOTS, 3, HEADS, GROUP])
        negm = sb("negm", [P, 2, 3, P], BF16)
        mT = sb("mT", [P, 2, NALL + 1], BF16)
        probs = sb("probs", [P, 4, 2 * NVIT])
        oT = sb("oT", [P, 2, NALL])
        rec = sb("rec", [P, 2, HEADS])
        on = sb("on", [P, 2 * DIM])
        onT = sb("onT", [P, NVIT])
        gT = att[:, 0:4 * NVIT].rearrange("p (s c n) -> p s c n", s=2, c=2)
        bn = sb("bn", [P, 3, 6])
        ag = sb("ag", [P, 3, 2])
        mv = sb("mv", [P, BATCH * 6])
        sd = sb("sd", [P, BATCH * 3])
        rs = sb("rs", [P, BATCH * 3])
        keys = k32[:, :, :].rearrange("p s n -> p (s n)")
        rr, s1, s2 = (keys[:, k * BATCH * 3:(k + 1) * BATCH * 3] for k in range(3))
        NG = BATCH * 3 * EXPERTS
        logit = att[:, 0:NG]
        gate = att[:, NG:2 * NG]
        ga = att[:, 2 * NG:3 * NG]
        gb = att[:, 3 * NG:4 * NG]
        hidT = att[:, 2 * NG:2 * NG + 8 * NALL].rearrange("p (s c n) -> p s c n", s=2, c=4)
        top = probs[:, :, :].rearrange("p s n -> p (s n)")[:, 0:6 * BATCH * 3].rearrange("p (k n) -> p k n", k=6)
        gnow = sb("gnow", [P, 3 * EXPERTS])
        gateT = qt[0:EXPERTS, 0, :]

        misc = [ctx.enter_context(nc.psum_tensor(f"misc{i}", [P, 512], F32)) for i in range(2)]
        plain = [ctx.enter_context(nc.psum_tensor(f"plain{i}", [P, 512], F32)) for i in range(2)]
        score = [ctx.enter_context(nc.psum_tensor(f"score{i}", [P, 512], F32)) for i in range(2)]
        outp = [ctx.enter_context(nc.psum_tensor(f"outp{i}", [P, 512], F32)) for i in range(2)]

        const_in = sem("const_in")
        txt_in = sem("txt_in")
        setup_v = sem("setup_v")
        img_in = [sem(f"img_in{i}") for i in range(2)]
        conv_done = sem("conv_done")
        conv_taken = sem("conv_taken")
        emb_done = sem("emb_done")
        emb_link = sem("emb_link")
        wa_in = sem("wa_in")
        wm_in = sem("wm_in")
        moe_in = sem("moe_in")
        sd_ready = sem("sd_ready")
        rs_ready = sem("rs_ready")
        fold_v = sem("fold_v")
        fold_pe = sem("fold_pe")
        fold_done = sem("fold_done")
        m_xn = sem("m_xn")
        m_t = sem("m_t")
        m_y = sem("m_y")
        m_f1 = sem("m_f1")
        m_g = sem("m_g")
        m_f2 = sem("m_f2")
        m_bias = sem("m_bias")
        m_link = sem("m_link")
        n_xn = sem("n_xn")
        n_w = sem("n_w")
        n_h = sem("n_h")
        n_link = sem("n_link")
        r_xn = sem("r_xn")
        r_t = sem("r_t")
        r_y = sem("r_y")
        r_l = sem("r_l")
        r_done = sem("r_done")
        g_v = sem("g_v")
        g_exp = sem("g_exp")
        e_xn = sem("e_xn")
        e_t = sem("e_t")
        e_y = sem("e_y")
        e_gt = sem("e_gt")
        e_gs = sem("e_gs")
        e_b2 = sem("e_b2")
        e_f1 = sem("e_f1")
        e_g = sem("e_g")
        e_f2 = sem("e_f2")
        e_acc = sem("e_acc")
        e_link = sem("e_link")
        out_done = sem("out_done")
        passed_v = sem("passed_v")
        passed_p = sem("passed_p")
        A = Attention(False, sem)
        X = Attention(True, sem)

        def h_tile(b, t, rows=None):
            return h[0:ROWS[t] if rows is None else rows, bass.ds(b * (3 * DIM) + t * DIM, DIM)]

        def h_image(b):
            return h[0:RT, bass.ds(b * (3 * DIM) + DIM, 2 * DIM)]

        def stat(array, b, t):
            return array[0:ROWS[t], bass.ds(b * 3 + t, 1)]

        def mean(b, t):
            return mv[0:ROWS[t], bass.ds(b * 6 + 2 * t, 1)]

        QUEUED = 6
        CONSTS = 19
        WA, WM = 4, 4

        block = ctx.enter_context(nc.Block())

        @block.sync
        def _(sp):
            def const(dst, src):
                sp.dma_start(dst, src).then_inc(const_in, 16)

            sp.wait_ge(setup_v, 1)
            with nc.allow_non_contiguous_dma(reason="small rows of constants"):
                const(ident[:, :], d["c_ident"])
                const(mask[:, :], d["c_mask"])
                const(rank[:, :], d["c_rank"].partition_broadcast(P))
                const(sel32[:, :], d["c_sel"])
                for half in range(2):
                    const(wconv[half * SHIFT:half * SHIFT + CROWS, :, :], d["conv_w"][half])
                const(on[0:RT, 0:DIM], d["pos"][0:RT, :])
                const(on[0:RT - 1, DIM:2 * DIM], d["pos"][RT:NTOK, :])
                const(probs[1:RT, 0, 0:DIM], d["conv_b"].partition_broadcast(RT - 1))
                const(probs[0:RT, 0, DIM:2 * DIM], d["conv_b"].partition_broadcast(RT))
                const(probs[0:1, 0, 0:DIM], d["cls"])
                const(wx[:, :], d["x_w"])
                for t in range(2):
                    const(norm_rows[0:RT, t, :], d["norm"][t].partition_broadcast(RT))
                const(vec_f[:, :], d["vec_f"])
                const(w_r[:, :], d["w_r"])
                const(b_r[0:RT, :], d["b_r"].partition_broadcast(RT))
                const(b2[0:EXPERTS, :], d["b2"])
                const(eps[:, :], d["c_eps"])
            sp.dma_start(h[0:TXT, :].rearrange("p (b t n) -> p b t n", b=BATCH, t=3)[:, :, 0, :],
                         d["txt"].rearrange("b p n -> p b n")).then_inc(txt_in, 16)

            def load_image(b, slot):
                img = imgs[slot].rearrange("p (g w) -> p g w", g=GRID)
                for half in range(2):
                    for c in range(3):
                        lo = half * SHIFT + c * PATCH
                        sp.dma_start(img[lo:lo + PATCH, :, 0:IMG - half * PIX],
                                     d["x"][bass.ds(b * 3 + c, 1), :, :, half * PIX:IMG]
                                     .rearrange("o p g w -> (o p) g w")).then_inc(img_in[slot], 16)

            for b in range(2):
                load_image(b, b)
            with sp.Fori(1, HALF) as i:
                for u in range(2):
                    sp.wait_ge(conv_done, i * 2 + (u - 1))
                    load_image(i * 2 + u, u)

            def load_attention(l):
                sp.dma_start(wqkv[:, :], d["qkv_w"][bass.ds(l, 1)].rearrange("o k n -> (o k) n")).then_inc(wa_in, 16)
                sp.dma_start(wproj[:, :], d["proj_w"][bass.ds(l, 1)].rearrange("o k n -> (o k) n")).then_inc(wa_in, 16)
                sp.dma_start(vec_a[:, :], d["vec"][bass.ds(l, 1), :, 0:5].rearrange("o k n -> (o k) n")).then_inc(wa_in, 16)
                sp.dma_start(row_a[0:RT, :], d["rows"][bass.ds(l * 2, 1), :].broadcast_to([RT, DIM])).then_inc(wa_in, 16)

            def load_mlp(l):
                sp.dma_start(wfc1[:, :], d["fc1_w"][bass.ds(l, 1)].rearrange("o k n -> (o k) n")).then_inc(wm_in, 16)
                sp.dma_start(wfc2[:, :, :], d["fc2_w"][bass.ds(l, 1)].rearrange("o (c k) n -> (o k) c n", c=2)).then_inc(wm_in, 16)
                sp.dma_start(vec_m[:, :], d["vec"][bass.ds(l, 1), :, 5:VBIAS].rearrange("o k n -> (o k) n")).then_inc(wm_in, 16)
                sp.dma_start(row_m[0:RT, :], d["rows"][bass.ds(l * 2 + 1, 1), :].broadcast_to([RT, DIM])).then_inc(wm_in, 16)

            with nc.allow_non_contiguous_dma(reason="small rows of constants"):
                load_attention(0)
                load_mlp(0)
                with sp.Fori(1, DEPTH) as l:
                    sp.wait_ge(A.link, l * (A.tail * BATCH))
                    load_attention(l)
                    sp.wait_ge(m_link, l * (4 * BATCH))
                    load_mlp(l)
            sp.wait_ge(conv_done, BATCH)
            sp.dma_start(w1, d["w1"].rearrange("e k f -> k e f")).then_inc(moe_in, 16)
            sp.dma_start(w2, d["w2"].rearrange("e (c k) n -> k e c n", c=4)).then_inc(moe_in, 16)
            with sp.Fori(0, BATCH) as b:
                sp.wait_ge(e_acc, b * EXPERTS + (EXPERTS + 2))
                for t, lo, rows in ((0, NTOK, TXT), (1, 0, RT), (2, RT, RT - 1)):
                    sp.dma_start(out[bass.ds(b, 1), lo:lo + rows, :].rearrange("o p n -> (o p) n"),
                                 h_tile(b, t, rows)).then_inc(out_done, 16)
            sp.wait_ge(out_done, 16 * 3 * BATCH)

        @block.tensor
        def _(pe):
            pe.wait_ge(const_in, 16 * CONSTS)
            pe.wait_ge(setup_v, 2)

            def conv(b, u, first):
                pe.wait_ge(img_in[u], (b + (2 - u)) * (8 * QUEUED))
                if not first:
                    pe.wait_ge(conv_taken, b - 1)
                img = imgs[u].rearrange("p (g x q) -> p g x q", g=GRID, q=PATCH)
                for q in range(PIX):
                    mm = pe.matmul(misc[u][:, 0:NPATCH], wconv[0:SHIFT + CROWS, q, :],
                                   img[0:SHIFT + CROWS, :, :, q], start=(q == 0), stop=(q == PIX - 1))
                mm.then_inc(conv_done, 1)

            def embed(b, u, first):
                pe.wait_ge(conv_taken, b + 1)
                if not first:
                    pe.wait_ge(emb_link, b * 7 - 13)
                for t in range(2):
                    mm = pe.transpose(plain[u][0:RT, t * DIM:(t + 1) * DIM],
                                      eT[:, u, t * RT:(t + 1) * RT], ident[:, :])
                mm.then_inc(emb_done, 1)

            conv(0, 0, True)
            conv(1, 1, True)
            embed(0, 0, True)
            embed(1, 1, True)
            with pe.Fori(1, HALF) as i:
                conv(i * 2, 0, False)
                conv(i * 2 + 1, 1, False)
                embed(i * 2, 0, False)
                embed(i * 2 + 1, 1, False)

            def project(T, s, base, names, wq, wk, wv):
                y = yT[:, s.u % 2, :]
                for name in names:
                    bank, at = bank_of(name, s)
                    pe.wait_ge(T.job_taken[bank], base * PHASE_JOBS + (at + 1))
                    if name == "T":
                        pe.wait_ge(T.xn_ready, base * BATCH + s.n + 1)
                        for t, (_, rows, _, col) in enumerate(T.tiles):
                            mm = pe.transpose(misc[bank][:, col:col + rows], xn[0:rows, s.u % 2, t, :],
                                              ident[0:rows, 0:rows])
                    elif name == "V":
                        for t, (_, rows, _, col) in enumerate(T.tiles):
                            mm = pe.matmul(misc[bank][0:rows, t * DIM:(t + 1) * DIM], y[:, col:col + rows], wv,
                                           start=True, stop=True)
                    else:
                        if name == "Q":
                            tbank, tat = bank_of("T", s)
                            pe.wait_ge(T.job_taken[tbank], base * PHASE_JOBS + (tat + 2))
                        mm = pe.matmul(misc[bank][:, 0:T.nq], wq if name == "Q" else wk, y[:, 0:T.nq],
                                       start=True, stop=True)
                    mm.then_inc(T.job_done[bank], 1)

            def plain_unit(T, s, base, w):
                if w == 0:
                    pe.wait_ge(T.qlow_ready, base * BATCH + s.n + 1)
                    pe.wait_ge(T.keys_ready, base * BATCH + T.last_kv(s).n + 1)
                if not (s.k == 0 and w < 2):
                    pe.wait_ge(T.max_taken, (base * BATCH + s.n) * T.units + (w - 1))
                _, rows, _, col = T.tiles[w // T.upt]
                q = qlow[s.u % 2][:, 0:HEADS * T.nq].rearrange("p (h n) -> p h n", h=HEADS)
                keys = klow[:, T.kv(s).u, 0:T.nk]
                for j in range(T.hpu):
                    mm = pe.matmul(plain[w % 2][0:rows, j * 256:j * 256 + T.nk],
                                   q[:, (w % T.upt) * T.hpu + j, col:col + rows], keys, start=True, stop=True)
                mm.then_inc(T.plain_ready, 1)

            def max_job(T, s, base):
                bank, at = bank_of("M", s)
                pe.wait_ge(T.job_taken[bank], base * PHASE_JOBS + (at + 1))
                pe.wait_ge(T.max_taken, (base * BATCH + s.n + 1) * T.units)
                low = misc[bank][:, :].bitcast(BF16)
                for t, (_, rows, _, col) in enumerate(T.tiles):
                    mm = pe.transpose(low[:, t * P:t * P + rows], negm[0:rows, s.u % 2, t, :],
                                      identb[0:rows, 0:rows])
                mm.then_inc(T.job_done[bank], 1)

            def score_unit(T, s, base, w):
                if w == 0:
                    pe.wait_ge(T.qhead_ready, base * BATCH + s.n + 1)
                    pe.wait_ge(T.keys_ready, base * BATCH + T.last_kv(s).n + 1)
                    bank, at = bank_of("M", s)
                    pe.wait_ge(T.job_taken[bank], base * PHASE_JOBS + (at + 2))
                if not (s.k == 0 and w < 2):
                    pe.wait_ge(T.exp_ready, (base * BATCH + s.n) * T.units + (w - 1))
                _, _, rows, col = T.tiles[w // T.upt]
                h0 = (w % T.upt) * T.hpu
                pe.matmul(score[w % 2][0:rows, 0:T.hpu * T.nq], k32[:, T.kv(s).u, col:col + rows],
                          qhead[s.u % 2][:, h0 * T.nq:(h0 + T.hpu) * T.nq], start=True, stop=False)
                for j in range(T.hpu):
                    mm = pe.matmul(score[w % 2][0:rows, j * T.nq:(j + 1) * T.nq], sel[:, h0 + j, 0:rows],
                                   mT[:, s.u % 2, 0:T.nq], start=False, stop=(j == T.hpu - 1))
                mm.then_inc(T.score_ready, 1)

            def value_unit(T, s, base, w):
                if w == 0:
                    bank, at = bank_of("V", T.kv(s))
                    pe.wait_ge(T.job_taken[bank], base * PHASE_JOBS + (at + 2))
                    pe.wait_ge(T.out_ready, base * BATCH + (s.n + 1))
                pe.wait_ge(T.exp_ready, (base * BATCH + s.n) * T.units + (w + 1))
                t = w // T.upt
                rows = T.tiles[t][2]
                for j in range(T.hpu):
                    hd = (w % T.upt) * T.hpu + j
                    lo = GROUP * (hd % 4)
                    mm = pe.matmul(outp[hd // 4][lo:lo + GROUP, 0:T.nq], vaug[0:rows, T.kv(s).u, t, hd, :],
                                   probs[0:rows, w % 4, j * T.nq:(j + 1) * T.nq],
                                   start=(t == 0), stop=(t == len(T.tiles) - 1), tile_position=(0, lo))
                mm.then_inc(T.pv_done, 1)

            def back(T, s, base, tiles, name):
                bank, at = bank_of(name, s)
                pe.wait_ge(T.job_taken[bank], base * PHASE_JOBS + (at + 1))
                pe.wait_ge(T.out_ready, base * BATCH + (s.n + 2))
                for k, t in enumerate(tiles):
                    _, rows, _, col = T.tiles[t]
                    for c in range(2):
                        mm = pe.transpose(misc[bank][0:rows, (2 * k + c) * P:(2 * k + c + 1) * P],
                                          oT[:, c, col:col + rows], ident[:, :])
                mm.then_inc(T.job_done[bank], 1)

            def end_job(T, s, base, j):
                name = f"E{j}"
                if T.cross:
                    back(T, s, base, [j], name)
                    return
                if j == 0:
                    back(T, s, base, [0, 1], name)
                    return
                bank, at = bank_of(name, s)
                pe.wait_ge(T.job_taken[bank], base * PHASE_JOBS + (at + 1))
                pbank, pat = bank_of(f"E{j - 1}", s)
                pe.wait_ge(T.job_taken[pbank], base * PHASE_JOBS + (pat + 2))
                for t in range(2):
                    if j == 1:
                        mm = pe.transpose(misc[bank][:, t * RT:(t + 1) * RT], on[0:RT, t * DIM:(t + 1) * DIM],
                                          ident[0:RT, 0:RT])
                    else:
                        mm = pe.matmul(misc[bank][0:RT, t * DIM:(t + 1) * DIM], onT[:, t * RT:(t + 1) * RT],
                                       wproj[:, :], start=True, stop=True)
                mm.then_inc(T.job_done[bank], 1)

            def attention(T, base, w_all):
                wq, wk, wv = (w_all[:, k * DIM:(k + 1) * DIM] for k in range(3))
                for m in range(LEAD):
                    project(T, Step(0, m), base, "TQKV", wq, wk, wv)
                for w in range(T.units):
                    plain_unit(T, Step(0, 0), base, w)
                max_job(T, Step(0, 0), base)

                def step(s):
                    ahead = s.k is None or s.k + LEAD < BATCH
                    more = s.k is None or s.k + 1 < BATCH
                    for w in range(T.units):
                        if w == 0 and ahead:
                            project(T, s.at(LEAD), base, "T", wq, wk, wv)
                        if w == 1 and s.k != 0:
                            end_job(T, s.at(-1), base, 0)
                        if w == 2 and ahead:
                            project(T, s.at(LEAD), base, "QKV", wq, wk, wv)
                        if w == 3 and s.k != 0:
                            end_job(T, s.at(-1), base, 1)
                        if w == 5 and s.k != 0:
                            end_job(T, s.at(-1), base, 2)
                        score_unit(T, s, base, w)
                        if w >= 2:
                            value_unit(T, s, base, w - 2)
                        if more:
                            for x in T.slots[w]:
                                plain_unit(T, s.at(1), base, x)
                    value_unit(T, s, base, T.units - 2)
                    if more:
                        max_job(T, s.at(1), base)
                    value_unit(T, s, base, T.units - 1)

                for u in range(SLOTS):
                    step(Step(0, u))
                with pe.Fori(1, BATCH // SLOTS - 1) as i:
                    for u in range(SLOTS):
                        step(Step(i, u))
                for u in range(SLOTS):
                    step(Step(BATCH // SLOTS - 1, u))
                for j in range(3):
                    end_job(T, Step(BATCH // SLOTS - 1, SLOTS - 1), base, j)

            def mlp(l):
                def turn(n, u):
                    pe.wait_ge(m_xn, l * BATCH + n + 1)
                    if isinstance(n, int):
                        if n > 1:
                            pe.wait_ge(m_y, l * BATCH + n - 1)
                    else:
                        pe.wait_ge(m_y, l * BATCH + n - 1)
                    for t in range(2):
                        mm = pe.transpose(misc[u][:, t * RT:(t + 1) * RT], xn[0:RT, u, t, :], ident[0:RT, 0:RT])
                    mm.then_inc(m_t, 1)

                def fc1(n, u, first=False):
                    pe.wait_ge(m_y, l * BATCH + n + 1)
                    if not first:
                        pe.wait_ge(m_g, l * BATCH + n - 1)
                    for c in range(2):
                        mm = pe.matmul(plain[u][:, c * NVIT:(c + 1) * NVIT], wfc1[:, c * P:(c + 1) * P],
                                       yT[:, u, 0:NVIT], start=True, stop=True)
                    mm.then_inc(m_f1, 1)

                def fc2(n, u, first=False):
                    pe.wait_ge(m_g, l * BATCH + n + 1)
                    if not first:
                        pe.wait_ge(m_link, (l * BATCH + n) * 4 - 7)
                    for t in range(2):
                        for c in range(2):
                            mm = pe.matmul(score[u][0:RT, t * DIM:(t + 1) * DIM], gT[:, u, c, t * RT:(t + 1) * RT],
                                           wfc2[:, c, :], start=(c == 0), stop=(c == 1))
                    mm.then_inc(m_f2, 1)

                turn(0, 0)
                turn(1, 1)
                fc1(0, 0, True)
                for n in range(2):
                    turn(n + 2, n)
                    fc1(n + 1, (n + 1) % 2, n == 0)
                    fc2(n, n, True)
                with pe.Fori(1, HALF - 1) as i:
                    for u in range(2):
                        turn(i * 2 + (u + 2), u)
                        fc1(i * 2 + (u + 1), (u + 1) % 2)
                        fc2(i * 2 + u, u)
                fc1(BATCH - 1, 1)
                fc2(BATCH - 2, 0)
                fc2(BATCH - 1, 1)

            with pe.Fori(0, DEPTH) as l:
                pe.wait_ge(wa_in, l * (16 * WA) + 16 * WA)
                pe.wait_ge(fold_v, l + 1)
                pe.matmul(plain[0][0:RT, 0:DIM], row_v[:, 0:RT], wproj[:, :], start=True, stop=True).then_inc(fold_pe, 1)
                pe.wait_ge(fold_done, l + 1)
                attention(A, l, wqkv)
                pe.wait_ge(wm_in, l * (16 * WM) + 16 * WM)
                mlp(l)
            attention(X, 0, wx)

            def turn_all(bank, slot, done):
                for t, (_, rows, _, col) in enumerate(X.tiles):
                    mm = pe.transpose(misc[bank][:, col:col + rows], xn[0:rows, slot, t, :], ident[0:rows, 0:rows])
                mm.then_inc(done, 1)

            def router_turn(n, u, first=False):
                pe.wait_ge(r_xn, n + 1)
                if not first:
                    pe.wait_ge(r_y, n - 1)
                turn_all(u, u, r_t)

            def router(n, u, first=False):
                pe.wait_ge(r_y, n + 1)
                if not first:
                    pe.wait_ge(r_done, n - 1)
                for t, (_, rows, _, col) in enumerate(X.tiles):
                    mm = pe.matmul(plain[u][0:rows, t * EXPERTS:(t + 1) * EXPERTS], yT[:, u, col:col + rows],
                                   w_r[:, :], start=True, stop=True)
                mm.then_inc(r_l, 1)

            router_turn(0, 0, True)
            router_turn(1, 1, True)
            router(0, 0, True)
            router_turn(2, 0)
            router(1, 1, True)
            with pe.Fori(1, HALF - 1) as i:
                router_turn(i * 2 + 1, 1)
                router(i * 2, 0)
                router_turn(i * 2 + 2, 0)
                router(i * 2 + 1, 1)
            router_turn(BATCH - 1, 1)
            router(BATCH - 2, 0)
            router(BATCH - 1, 1)

            def expert_turn(n):
                pe.wait_ge(e_xn, n + 1)
                turn_all(0, 0, e_t)

            def fc1_chunk(n, e, c):
                pe.wait_ge(e_g, n * 32 + (4 * e + c + 1))
                pe.matmul(plain[c % 2][:, 0:NALL], w1[:, e, c * P:(c + 1) * P], yT[:, 0, 0:NALL],
                          start=True, stop=True).then_inc(e_f1, 1)

            def fc2_expert(n, e):
                pe.wait_ge(e_g, n * 32 + (4 * e + 6))
                pe.wait_ge(e_acc, n * 8 + (e + 1))
                for t, (_, rows, _, col) in enumerate(X.tiles):
                    for c in range(4):
                        mm = pe.matmul(score[e % 2][0:rows, t * DIM:(t + 1) * DIM],
                                       hidT[:, e % 2, c, col:col + rows], w2[:, e, c, :],
                                       start=(c == 0), stop=(c == 3))
                mm.then_inc(e_f2, 1)

            def experts(n, more):
                pe.wait_ge(e_y, n + 1)
                for e in range(EXPERTS):
                    for c in range(4):
                        fc1_chunk(n, e, c)
                    if e == 1:
                        pe.wait_ge(e_link, n * 3 + 1)
                        for t, (_, rows, _, col) in enumerate(X.tiles):
                            mm = pe.transpose(misc[1][0:EXPERTS, col:col + rows],
                                              gnow[0:rows, t * EXPERTS:(t + 1) * EXPERTS],
                                              ident[0:rows, 0:rows])
                        mm.then_inc(e_gt, 1)
                    if e == 2:
                        pe.wait_ge(e_gs, n + 1)
                        for t, (_, rows, _, col) in enumerate(X.tiles):
                            mm = pe.matmul(misc[1][0:rows, t * DIM:(t + 1) * DIM], gateT[0:EXPERTS, col:col + rows],
                                           b2[0:EXPERTS, :], start=True, stop=True)
                        mm.then_inc(e_b2, 1)
                    if e == 4 and more:
                        expert_turn(n + 1)
                    if e:
                        fc2_expert(n, e - 1)
                fc2_expert(n, EXPERTS - 1)

            pe.wait_ge(moe_in, 32)
            expert_turn(0)
            with pe.Fori(0, BATCH - 1) as b:
                experts(b, True)
            experts(BATCH - 1, False)

        @block.scalar
        def _(act):
            act.wait_ge(const_in, 16 * CONSTS)
            act.wait_ge(setup_v, 2)
            with act.Fori(0, HALF) as i:
                for u in range(2):
                    act.wait_ge(conv_done, i * 2 + (u + 1))
                    act.activation(eT[:, u, 1:1 + NPATCH], misc[u][:, 0:NPATCH], ACT.Copy).then_inc(conv_taken, 1)

            def deviation(src):
                act.activation(sd[0:RT, :], src, ACT.Sqrt, bias=eps[0:RT, :]).then_inc(sd_ready, 1)

            variances = mv[0:RT, :].rearrange("p (n s) -> p n s", s=2)[:, :, 1]

            def take(T, s, base, name):
                bank, at = bank_of(name, s)
                act.wait_ge(T.job_done[bank], base * PHASE_JOBS + (at + 1))
                return misc[bank], T.job_taken[bank]

            def take_turned(T, s, base):
                ps, taken = take(T, s, base, "T")
                y = yT[:, s.u % 2, 0:T.nq]
                if T.cross:
                    act.activation(y, ps[:, 0:T.nq], ACT.Copy).then_inc(taken, 1)
                else:
                    act.activation(y, ps[:, 0:T.nq], ACT.Identity, bias=vec_a[:, 1:2],
                                   scale=vec_a[:, 0:1]).then_inc(taken, 1)

            def take_query(T, s, base, used):
                if used:
                    act.wait_ge(T.qhead_ready, base * BATCH + s.n - 1)
                    act.wait_ge(T.qlow_ready, base * BATCH + s.n - 1)
                ps, taken = take(T, s, base, "Q")
                q = qt[:, s.u % 2, 0:T.nq]
                if T.cross:
                    act.activation(q, ps[:, 0:T.nq], ACT.Copy, scale=float(DIM) ** -0.5).then_inc(taken, 1)
                else:
                    act.activation(q, ps[:, 0:T.nq], ACT.Identity, bias=qbias[:, :],
                                   scale=float(HD) ** -0.5).then_inc(taken, 1)

            def take_value(T, s, base):
                ps, taken = take(T, s, base, "V")
                v = ps[:, 0:len(T.tiles) * DIM].rearrange("p (t h d) -> p t h d", t=len(T.tiles), h=HEADS)
                first = 0
                if T.cross:
                    act.activation(vaug[0:TXT, s.u, 0, :, 0:HD], v[0:TXT, 0], ACT.Copy)
                    first = 1
                act.activation(vaug[0:RT, s.u, first:first + 2, :, 0:HD], v[0:RT, first:first + 2],
                               ACT.Copy).then_inc(taken, 1)

            def take_max(T, s, base):
                ps, taken = take(T, s, base, "M")
                low = ps[:, :].bitcast(BF16)
                first, col = 0, 0
                if T.cross:
                    act.activation(mT[:, s.u % 2, 0:TXT], low[:, 0:TXT], ACT.Copy)
                    first, col = 1, TXT
                act.activation(mT[:, s.u % 2, col:col + 2 * RT].rearrange("p (t n) -> p t n", t=2),
                               low[:, first * P:(first + 2) * P].rearrange("p (t n) -> p t n", t=2)[:, :, 0:RT],
                               ACT.Copy).then_inc(taken, 1)

            def take_output(T, s, base):
                act.wait_ge(T.pv_done, (base * BATCH + (s.n + 1)) * T.units)
                for c in range(2):
                    ins = act.activation(oT[:, c, 0:T.nq], outp[c][:, 0:T.nq], ACT.Copy)
                ins.then_inc(T.out_ready, 1)

            def exp_unit(T, s, base, w):
                act.wait_ge(T.score_ready, (base * BATCH + s.n) * T.units + (w + 1))
                if not (s.k == 0 and w < 4):
                    act.wait_ge(T.pv_done, (base * BATCH + s.n) * T.units + (w - 3))
                rows = T.tiles[w // T.upt][2]
                act.activation(probs[0:rows, w % 4, 0:T.hpu * T.nq], score[w % 2][0:rows, 0:T.hpu * T.nq],
                               ACT.Exp).then_inc(T.exp_ready, 1)

            def attention(T, base):
                for m in range(LEAD):
                    take_turned(T, Step(0, m), base)
                    take_query(T, Step(0, m), base, False)
                    take_value(T, Step(0, m), base)
                take_max(T, Step(0, 0), base)

                def step(s):
                    ahead = s.k is None or s.k + LEAD < BATCH
                    for w in range(T.units):
                        if w == 0 and ahead:
                            take_turned(T, s.at(LEAD), base)
                        if w == 2 and ahead:
                            take_query(T, s.at(LEAD), base, True)
                            take_value(T, s.at(LEAD), base)
                        if w == 3 and s.k != 0 and not T.cross:
                            take_heads(T, s.at(-1), base)
                        exp_unit(T, s, base, w)
                    if s.k is None or s.k + 1 < BATCH:
                        take_max(T, s.at(1), base)
                    take_output(T, s, base)

                def take_heads(T, s, base):
                    ps, taken = take(T, s, base, "E1")
                    act.activation(onT[:, :], ps[:, 0:NVIT], ACT.Copy).then_inc(taken, 1)

                for u in range(SLOTS):
                    step(Step(0, u))
                with act.Fori(1, BATCH // SLOTS - 1) as i:
                    for u in range(SLOTS):
                        step(Step(i, u))
                for u in range(SLOTS):
                    step(Step(BATCH // SLOTS - 1, u))
                if not T.cross:
                    take_heads(T, Step(BATCH // SLOTS - 1, SLOTS - 1), base)

            def mlp(l):
                def norm(n, u):
                    act.wait_ge(m_t, l * BATCH + n + 1)
                    act.activation(yT[:, u, 0:NVIT], misc[u][:, 0:NVIT], ACT.Identity, bias=vec_m[:, 1:2],
                                   scale=vec_m[:, 0:1]).then_inc(m_y, 1)

                def gelu(n, u):
                    act.wait_ge(m_f1, l * BATCH + n + 1)
                    for c in range(2):
                        ins = act.activation(gT[:, u, c, :], plain[u][:, c * NVIT:(c + 1) * NVIT], ACT.Gelu,
                                             bias=vec_m[:, 2 + c:3 + c])
                    ins.then_inc(m_g, 1)

                norm(0, 0)
                norm(1, 1)
                gelu(0, 0)
                with act.Fori(0, HALF - 1) as i:
                    for u in range(2):
                        norm(i * 2 + (u + 2), u)
                        gelu(i * 2 + (u + 1), (u + 1) % 2)
                gelu(BATCH - 1, 1)

            act.wait_ge(emb_link, 7 * BATCH)
            deviation(variances)
            with act.Fori(0, DEPTH) as l:
                act.wait_ge(fold_done, l + 1)
                attention(A, l)
                act.wait_ge(A.link, l * (A.tail * BATCH) + A.tail * BATCH)
                deviation(variances)
                act.wait_ge(wm_in, l * (16 * WM) + 16 * WM)
                mlp(l)
                act.wait_ge(m_link, l * (4 * BATCH) + 4 * BATCH)
                deviation(variances)
            act.wait_ge(n_link, 3 * BATCH)
            deviation(variances)
            attention(X, 0)
            act.wait_ge(X.link, X.tail * BATCH)
            deviation(variances)
            act.wait_ge(g_v, 1)
            deviation(s1[0:RT, :])

            def router_norm(n, u):
                act.wait_ge(r_t, n + 1)
                act.activation(yT[:, u, 0:NALL], misc[u][:, 0:NALL], ACT.Identity, bias=vec_f[:, 1:2],
                               scale=vec_f[:, 0:1]).then_inc(r_y, 1)

            with act.Fori(0, HALF) as i:
                for u in range(2):
                    router_norm(i * 2 + u, u)
            act.wait_ge(g_v, G_EXP)
            act.activation(top[0:RT, 3, :], top[0:RT, 2, :], ACT.Exp).then_inc(g_exp, 1)

            def expert_norm(n):
                act.wait_ge(e_t, n + 1)
                act.activation(yT[:, 0, 0:NALL], misc[0][:, 0:NALL], ACT.Identity, bias=vec_f[:, 1:2],
                               scale=vec_f[:, 0:1]).then_inc(e_y, 1)

            def expert_gelus(n):
                for e in range(EXPERTS):
                    for c in range(4):
                        act.wait_ge(e_f1, n * 32 + (4 * e + c + 1))
                        act.activation(hidT[:, e % 2, c, :], plain[c % 2][:, 0:NALL], ACT.Gelu,
                                       bias=vec_f[:, 2 + 4 * e + c:3 + 4 * e + c]).then_inc(e_g, 1)

            act.wait_ge(g_v, G_ALL)
            expert_norm(0)
            with act.Fori(0, BATCH - 1) as b:
                expert_gelus(b)
                expert_norm(b + 1)
            expert_gelus(BATCH - 1)

        @block.vector
        def _(dve):
            dve.memset(big[32:64, 0:2 * GRID * IMG], 0.0)
            dve.memset(wconv[32:64, :, :], 0.0)
            dve.memset(on[:, :], 0.0).then_inc(setup_v, 1)
            dve.memset(vaug[:, :, :, :, :], 1.0)
            dve.memset(negm[:, :, :, :], 0.0)
            dve.memset(mv[:, :], 1.0)
            dve.memset(eT[:, :, :], 0.0)
            dve.memset(gnow[:, :], 0.0).then_inc(e_g, 1)
            dve.memset(gateT[:, :], 0.0).then_inc(e_g, 1)
            dve.memset(rec[:, :, :], 0.0).then_inc(e_acc, 1)
            dve.memset(bn[:, :, :], 0.0).then_inc(e_acc, 1)
            for T in (A, X):
                for free in (*T.job_taken, T.out_ready):
                    dve.sem_inc(free, 1)
            dve.wait_ge(const_in, 16 * CONSTS)
            dve.tensor_copy(identb[:, :], ident[:, :])
            dve.tensor_copy(sel[:, :, :], sel32[:, :].unsqueeze(2).to_broadcast([P, HEADS, RT]))
            dve.tensor_tensor(posb[0:RT, :, :], on[0:RT, :].rearrange("p (t n) -> p t n", t=2),
                              probs[0:RT, 0, 0:2 * DIM].rearrange("p (t n) -> p t n", t=2),
                              ALU.add).then_inc(setup_v, 1)
            dve.wait_ge(setup_v, 2)
            dve.wait_ge(txt_in, 16)

            def stats(b, tiles, link, v):
                dve.sem_inc(passed_v, 1)
                for t in tiles:
                    ins = dve.bn_stats(bn[0:ROWS[t], t, :], h_tile(b, t))
                ins.then_inc(link, 1)
                dve.wait_ge(link, v + 1)
                dve.sem_inc(passed_v, 1)
                for t in tiles:
                    ins = dve.bn_aggr(ag[0:ROWS[t], t, :], bn[0:ROWS[t], t, :])
                ins.then_inc(link, 1)
                dve.wait_ge(link, v + 2)
                t0, rows = tiles[0], ROWS[tiles[0]]
                dve.tensor_copy(mv[0:rows, bass.ds(b * 6 + 2 * t0, 2 * len(tiles))],
                                ag[0:rows, t0:t0 + len(tiles), :].rearrange("p t s -> p (t s)")).then_inc(link, 1)

            with dve.Fori(0, HALF) as i:
                for u in range(2):
                    b = i * 2 + u
                    dve.wait_ge(emb_done, b + 1)
                    dve.tensor_tensor(h_image(b), plain[u][0:RT, 0:2 * DIM],
                                      posb[0:RT, :, :].rearrange("p t n -> p (t n)"), ALU.add).then_inc(emb_link, 1)
                    dve.wait_ge(emb_link, b * 7 + 1)
                    stats(b, [1, 2], emb_link, b * 7 + 1)
                    stats(b, [0], emb_link, b * 7 + 4)

            def invert(count):
                dve.wait_ge(sd_ready, count)
                dve.reciprocal(rs[0:RT, :], sd[0:RT, :]).then_inc(rs_ready, 1)
                dve.wait_ge(rs_ready, count)

            def normalise(b, slot, tiles, scale):
                for k, t in enumerate(tiles):
                    ins = dve.tensor_scalar(xn[0:ROWS[t], slot, k, :], h_tile(b, t), mean(b, t), stat(scale, b, t),
                                            ALU.subtract, ALU.mult)
                return ins

            def take(T, s, base, name):
                bank, at = bank_of(name, s)
                dve.wait_ge(T.job_done[bank], base * PHASE_JOBS + (at + 1))
                return misc[bank], T.job_taken[bank], base * PHASE_JOBS + (at + 2)

            def norm_rows_of(T, s, base, wait):
                if wait:
                    bank, at = bank_of("T", s.at(-2))
                    dve.wait_ge(T.job_done[bank], base * PHASE_JOBS + (at + 1))
                normalise(s.sample, s.u % 2, [t[0] for t in T.tiles], rs).then_inc(T.xn_ready, 1)

            def take_keys(T, s, base):
                ps, taken, count = take(T, s, base, "K")
                if T.cross:
                    dve.tensor_copy(k32[:, s.u, 0:T.nq], ps[:, 0:T.nq]).then_inc(taken, 1)
                else:
                    dve.tensor_scalar(k32[:, s.u, 0:T.nq], ps[:, 0:T.nq], vec_a[:, 3:4], None,
                                      ALU.add).then_inc(taken, 1)
                dve.wait_ge(taken, count)
                dve.tensor_copy(klow[:, s.u, 0:T.nq], k32[:, s.u, 0:T.nq]).then_inc(T.keys_ready, 1)

            def low_queries(T, s, base):
                bank, at = bank_of("Q", s)
                dve.wait_ge(T.job_taken[bank], base * PHASE_JOBS + (at + 2))
                shape = [P, HEADS, T.nq]
                dve.tensor_tensor(qlow[s.u % 2][:, 0:HEADS * T.nq].rearrange("p (h n) -> p h n", h=HEADS),
                                  qt[:, s.u % 2, 0:T.nq].unsqueeze(1).to_broadcast(shape),
                                  mask[:, :].unsqueeze(2).to_broadcast(shape), ALU.mult).then_inc(T.qlow_ready, 1)

            def max_unit(T, s, base, w):
                dve.wait_ge(T.plain_ready, (base * BATCH + s.n) * T.units + (w + 1))
                t = w // T.upt
                rows = T.tiles[t][1]
                h0 = (w % T.upt) * T.hpu
                src = plain[w % 2][0:rows, :].rearrange("p (j n) -> p j n", j=2)[:, :, 0:T.nk] if T.hpu == 2 \
                    else plain[w % 2][0:rows, 0:T.nk].unsqueeze(1)
                dve.tensor_reduce(negm[0:rows, s.u % 2, t, h0:h0 + T.hpu], src, AX.X, ALU.max,
                                  negate=True).then_inc(T.max_taken, 1)

            def end_image(T, s, base):
                ps, taken, _ = take(T, s, base, "E0")
                v = base * (T.tail * BATCH) + s.n * T.tail
                o = ps[0:RT, 0:512].rearrange("p (t h x) -> p t h x", t=2, h=HEADS)
                dve.reciprocal(rec[0:RT, :, :].unsqueeze(3), o[:, :, :, HD:HD + 1]).then_inc(T.link, 1)
                dve.wait_ge(T.link, v + 1)
                dve.tensor_tensor(on[0:RT, :].rearrange("p (t h d) -> p t h d", t=2, h=HEADS), o[:, :, :, 0:HD],
                                  rec[0:RT, :, :].unsqueeze(3).to_broadcast([RT, 2, HEADS, HD]),
                                  ALU.mult).then_inc(taken, 1)

            def end_projected(T, s, base):
                ps, taken, count = take(T, s, base, "E2")
                dve.wait_ge(T.bias_added, base * BATCH + s.n + 1)
                b = s.sample
                dve.tensor_tensor(h_image(b), ps[0:RT, 0:2 * DIM], h_image(b), ALU.add).then_inc(taken, 1)
                dve.wait_ge(taken, count)
                stats(b, [1, 2], T.link, base * (T.tail * BATCH) + s.n * T.tail + 1)

            def end_cross(T, s, base, j):
                ps, taken, count = take(T, s, base, f"E{j}")
                v = s.n * T.tail + 5 * j
                t, rows, _, _ = T.tiles[j]
                o = ps[0:rows, 0:256].rearrange("p (h x) -> p h x", h=HEADS)
                dve.reciprocal(rec[0:rows, 0, :].unsqueeze(2), o[:, :, HD:HD + 1]).then_inc(T.link, 1)
                dve.wait_ge(T.link, v + 1)
                dve.tensor_tensor(on[0:rows, 0:DIM].rearrange("p (d h) -> p h d", h=HEADS), o[:, :, 0:HD],
                                  rec[0:rows, 0, :].unsqueeze(2).to_broadcast([rows, HEADS, HD]),
                                  ALU.mult).then_inc(taken, 1)
                dve.wait_ge(taken, count)
                b = s.sample
                dve.tensor_tensor(h_tile(b, t), h_tile(b, t), on[0:rows, 0:DIM], ALU.add).then_inc(T.link, 1)
                dve.wait_ge(T.link, v + 2)
                stats(b, [t], T.link, v + 2)

            def attention(T, base):
                for m in range(LEAD):
                    norm_rows_of(T, Step(0, m), base, False)
                for m in range(LEAD):
                    take_keys(T, Step(0, m), base)
                    low_queries(T, Step(0, m), base)
                norm_rows_of(T, Step(0, LEAD), base, True)
                for w in range(T.units):
                    max_unit(T, Step(0, 0), base, w)

                def step(s):
                    inner = s.k is None
                    for w in range(T.units):
                        if w == 1 and s.k != 0:
                            if T.cross:
                                end_cross(T, s.at(-1), base, 0)
                            else:
                                end_image(T, s.at(-1), base)
                        if w == 2 and (inner or s.k + LEAD < BATCH):
                            take_keys(T, s.at(LEAD), base)
                        if w == 3:
                            if T.cross and s.k != 0:
                                end_cross(T, s.at(-1), base, 1)
                            if inner or s.k + LEAD < BATCH:
                                low_queries(T, s.at(LEAD), base)
                        if w == 5 and s.k != 0:
                            if T.cross:
                                end_cross(T, s.at(-1), base, 2)
                            else:
                                end_projected(T, s.at(-1), base)
                        if w == 6 and (inner or s.k + LEAD + 1 < BATCH):
                            norm_rows_of(T, s.at(LEAD + 1), base, True)
                        if inner or s.k + 1 < BATCH:
                            for x in T.slots[w]:
                                max_unit(T, s.at(1), base, x)

                for u in range(SLOTS):
                    step(Step(0, u))
                with dve.Fori(1, BATCH // SLOTS - 1) as i:
                    for u in range(SLOTS):
                        step(Step(i, u))
                for u in range(SLOTS):
                    step(Step(BATCH // SLOTS - 1, u))
                last = Step(BATCH // SLOTS - 1, SLOTS - 1)
                if T.cross:
                    for j in range(3):
                        end_cross(T, last, base, j)
                else:
                    end_image(T, last, base)
                    end_projected(T, last, base)

            def mlp(l):
                def norm(n, u, wait=True):
                    if wait:
                        dve.wait_ge(m_t, l * BATCH + n - 1)
                    normalise(n, u, [1, 2], rs).then_inc(m_xn, 1)

                def residual(n, u):
                    v = (l * BATCH + n) * 4
                    dve.wait_ge(m_f2, l * BATCH + n + 1)
                    dve.wait_ge(m_bias, l * BATCH + n + 1)
                    dve.tensor_tensor(h_image(n), score[u][0:RT, 0:2 * DIM], h_image(n), ALU.add).then_inc(m_link, 1)
                    dve.wait_ge(m_link, v + 1)
                    stats(n, [1, 2], m_link, v + 1)

                norm(0, 0, False)
                norm(1, 1, False)
                norm(2, 0)
                with dve.Fori(0, HALF - 2) as i:
                    for u in range(2):
                        norm(i * 2 + (u + 3), (u + 1) % 2)
                        residual(i * 2 + u, u)
                norm(BATCH - 1, 1)
                for n in range(BATCH - 4, BATCH):
                    residual(n, n % 2)

            with dve.Fori(0, DEPTH) as l:
                dve.wait_ge(wa_in, l * (16 * WA) + 16 * WA)
                dve.tensor_scalar(row_v[:, :], ident[:, :], 0.0, vec_a[:, 4:5], ALU.mult, ALU.add)
                dve.tensor_scalar(qbias[:, :], vec_a[:, 2:3], float(HD) ** -0.5, None, ALU.mult).then_inc(fold_v, 1)
                dve.wait_ge(fold_pe, l + 1)
                dve.tensor_tensor(row_a[0:RT, :], plain[0][0:RT, 0:DIM], row_a[0:RT, :], ALU.add).then_inc(fold_done, 1)
                invert(l * 2 + 1)
                attention(A, l)
                invert(l * 2 + 2)
                mlp(l)
            invert(2 * DEPTH + 1)

            def final_norm(n):
                for t in (1, 2):
                    ins = dve.tensor_scalar(h_tile(n, t), h_tile(n, t), mean(n, t), stat(rs, n, t),
                                            ALU.subtract, ALU.mult)
                ins.then_inc(n_xn, 1)

            def final_stats(n):
                dve.wait_ge(n_h, n + 1)
                stats(n, [1, 2], n_link, n * 3)

            final_norm(0)
            final_norm(1)
            with dve.Fori(0, BATCH - 2) as b:
                final_norm(b + 2)
                final_stats(b)
            final_stats(BATCH - 2)
            final_stats(BATCH - 1)
            invert(2 * DEPTH + 2)
            attention(X, 0)
            invert(2 * DEPTH + 3)

            count = [0]

            def link(ins):
                count[0] += 1
                ins.then_inc(g_v, 1)
                dve.wait_ge(g_v, count[0])

            r, r2 = rs[0:RT, :], rr[0:RT, :]
            pairs = mv[0:RT, :].rearrange("p (n s) -> p n s", s=2)
            dve.tensor_tensor(s2[0:RT, :], pairs[:, :, 1], r, ALU.mult).then_inc(fold_v, 1)
            dve.wait_ge(fold_v, DEPTH + 1)
            link(dve.tensor_tensor(s1[0:RT, :], s2[0:RT, :], r, ALU.mult))
            dve.wait_ge(sd_ready, 2 * DEPTH + 4)
            link(dve.reciprocal(s2[0:RT, :], sd[0:RT, :]))
            link(dve.tensor_tensor(r2, s2[0:RT, :], r, ALU.mult))
            link(dve.tensor_scalar(s1[0:RT, :], r, 1.0, None, ALU.add))
            link(dve.tensor_tensor(s2[0:RT, :], pairs[:, :, 0], r, ALU.mult))
            link(dve.memset(logit[:, :], 0.0))

            def router_rows(n, u, wait=True):
                if wait:
                    dve.wait_ge(r_t, n - 1)
                normalise(n, u, range(3), rr).then_inc(r_xn, 1)

            def router_logits(n, u):
                dve.wait_ge(r_l, n + 1)
                for lo, k, rows in ((0, 1, TXT), (1, 2, RT)):
                    ins = dve.tensor_tensor(
                        logit[0:rows, bass.ds(n * 24 + lo * EXPERTS, k * EXPERTS)],
                        plain[u][0:rows, lo * EXPERTS:(lo + k) * EXPERTS], br2[0:rows, 0:k * EXPERTS], ALU.add)
                ins.then_inc(r_done, 1)

            for k in range(2):
                ins = dve.tensor_copy(br2[0:RT, k * EXPERTS:(k + 1) * EXPERTS], b_r[0:RT, :])
            link(ins)
            router_rows(0, 0, False)
            router_rows(1, 1, False)
            router_rows(2, 0)
            router_logits(0, 0)
            with dve.Fori(0, HALF - 2) as i:
                router_rows(i * 2 + 3, 1)
                router_logits(i * 2 + 1, 1)
                router_rows(i * 2 + 4, 0)
                router_logits(i * 2 + 2, 0)
            router_rows(BATCH - 1, 1)
            for n in range(BATCH - 3, BATCH):
                router_logits(n, n % 2)
            dve.wait_ge(r_done, BATCH)

            n3 = BATCH * 3
            cube = lambda a: a[0:RT, :].rearrange("p (n e) -> p n e", e=EXPERTS)
            wide = lambda k: top[0:RT, k, :].unsqueeze(2).to_broadcast([RT, n3, EXPERTS])
            ranks = rank[0:RT, :].unsqueeze(1).to_broadcast([RT, n3, EXPERTS])
            L, G, TA, TB = cube(logit), cube(gate), cube(ga), cube(gb)

            def pick(src, best, first, chosen):
                link(dve.tensor_reduce(top[0:RT, best, :], src, AX.X, ALU.max))
                link(dve.tensor_tensor(chosen, src, wide(best), ALU.is_equal))
                link(dve.tensor_tensor(chosen, chosen, ranks, ALU.mult))
                link(dve.tensor_reduce(top[0:RT, first, :], chosen, AX.X, ALU.max))
                link(dve.tensor_tensor(chosen, chosen, wide(first), ALU.is_equal))

            pick(L, 0, 4, TA)
            link(dve.scalar_tensor_tensor(out=L, in0=TA, scalar=-3.0e38, in1=L, op0=ALU.mult, op1=ALU.add))
            pick(L, 1, 5, TB)
            link(dve.tensor_tensor(top[0:RT, 2, :], top[0:RT, 1, :], top[0:RT, 0, :], ALU.subtract))
            assert count[0] == G_EXP
            dve.wait_ge(g_exp, 1)
            link(dve.tensor_scalar(top[0:RT, 4, :], top[0:RT, 3, :], 1.0, None, ALU.add))
            link(dve.reciprocal(top[0:RT, 0, :], top[0:RT, 4, :]))
            link(dve.tensor_tensor(top[0:RT, 1, :], top[0:RT, 3, :], top[0:RT, 0, :], ALU.mult))
            link(dve.tensor_tensor(TA, TA, wide(0), ALU.mult))
            link(dve.tensor_tensor(TB, TB, wide(1), ALU.mult))
            link(dve.tensor_tensor(G, TA, TB, ALU.add))
            assert count[0] == G_ALL

            def expert_rows(n):
                normalise(n, 0, range(3), rr).then_inc(e_xn, 1)

            def experts(n, more):
                dve.wait_ge(e_acc, n * EXPERTS + 2)
                dve.sem_inc(passed_v, 1)
                dve.tensor_copy(gnow[0:RT, :], gate[0:RT, bass.ds(n * 24, 24)]).then_inc(e_link, 1)
                dve.wait_ge(e_link, n * 3 + 1)
                for t in range(3):
                    ins = dve.tensor_scalar(h_tile(n, t), h_tile(n, t), stat(s1, n, t), stat(s2, n, t),
                                            ALU.mult, ALU.subtract)
                ins.then_inc(e_link, 1)
                dve.wait_ge(e_gt, n + 1)
                dve.tensor_copy(gateT[:, :], misc[1][0:EXPERTS, 0:NALL]).then_inc(e_gs, 1)
                dve.wait_ge(e_b2, n + 1)
                dve.wait_ge(e_link, n * 3 + 2)
                dve.tensor_tensor(h_tile(n, 0), misc[1][0:TXT, 0:DIM], h_tile(n, 0), ALU.add)
                dve.tensor_tensor(h_image(n), misc[1][0:RT, DIM:3 * DIM], h_image(n), ALU.add).then_inc(e_link, 1)
                dve.wait_ge(e_link, n * 3 + 3)
                for e in range(EXPERTS):
                    if e == 3 and more:
                        dve.wait_ge(e_t, n + 1)
                        expert_rows(n + 1)
                    dve.wait_ge(e_f2, n * EXPERTS + (e + 1))
                    dve.wait_ge(e_acc, n * EXPERTS + (e + 2))
                    for t in range(3):
                        ins = dve.scalar_tensor_tensor(
                            out=h_tile(n, t), in0=score[e % 2][0:ROWS[t], t * DIM:(t + 1) * DIM],
                            scalar=gnow[0:ROWS[t], t * EXPERTS + e:t * EXPERTS + e + 1], in1=h_tile(n, t),
                            op0=ALU.mult, op1=ALU.add)
                    ins.then_inc(e_acc, 1)

            expert_rows(0)
            with dve.Fori(0, BATCH - 1) as b:
                experts(b, True)
            experts(BATCH - 1, False)

        @block.gpsimd
        def _(pool):
            pool.wait_ge(const_in, 16 * CONSTS)

            def head_queries(T, s, base):
                if s.k is None or s.k > 1:
                    pool.wait_ge(T.score_ready, (base * BATCH + s.n - 1) * T.units)
                bank, at = bank_of("Q", s)
                pool.wait_ge(T.job_taken[bank], base * PHASE_JOBS + (at + 2))
                shape = [P, HEADS, T.nq]
                pool.tensor_tensor(qhead[s.u % 2][:, 0:HEADS * T.nq].rearrange("p (h n) -> p h n", h=HEADS),
                                   qt[:, s.u % 2, 0:T.nq].unsqueeze(1).to_broadcast(shape),
                                   mask[:, :].unsqueeze(2).to_broadcast(shape), ALU.mult).then_inc(T.qhead_ready, 1)

            def add_bias(b, row):
                pool.sem_inc(passed_p, 1)
                image = h_image(b).rearrange("p (t n) -> p t n", t=2)
                return pool.tensor_tensor(image, image, row.unsqueeze(1).to_broadcast([RT, 2, DIM]), ALU.add)

            def add_output_bias(T, s, base):
                if T.cross:
                    return
                pool.wait_ge(T.xn_ready, base * BATCH + s.n + 1)
                add_bias(s.sample, row_a[0:RT, :]).then_inc(T.bias_added, 1)

            def attention(T, base):
                head_queries(T, Step(0, 0), base)
                for m in range(LEAD):
                    add_output_bias(T, Step(0, m), base)

                def step(s):
                    if s.k is None or s.k + 1 < BATCH:
                        head_queries(T, s.at(1), base)
                    if s.k is None or s.k + LEAD < BATCH:
                        add_output_bias(T, s.at(LEAD), base)

                for u in range(SLOTS):
                    step(Step(0, u))
                with pool.Fori(1, BATCH // SLOTS - 1) as i:
                    for u in range(SLOTS):
                        step(Step(i, u))
                for u in range(SLOTS):
                    step(Step(BATCH // SLOTS - 1, u))

            with pool.Fori(0, DEPTH) as l:
                pool.wait_ge(fold_done, l + 1)
                attention(A, l)
                pool.wait_ge(wm_in, l * (16 * WM) + 16 * WM)
                pool.sem_inc(passed_p, 1)
                with pool.Fori(0, BATCH) as b:
                    pool.wait_ge(m_xn, l * BATCH + b + 1)
                    add_bias(b, row_m[0:RT, :]).then_inc(m_bias, 1)
            with pool.Fori(0, BATCH) as b:
                pool.wait_ge(n_xn, b + 1)
                pool.sem_inc(passed_p, 1)
                image = h_image(b).rearrange("p (t n) -> p t n", t=2)
                wide = [RT, 2, DIM]
                pool.tensor_tensor(image, image, norm_rows[0:RT, 0, :].unsqueeze(1).to_broadcast(wide),
                                   ALU.mult).then_inc(n_w, 1)
                pool.wait_ge(n_w, b + 1)
                pool.sem_inc(passed_p, 1)
                pool.tensor_tensor(image, image, norm_rows[0:RT, 1, :].unsqueeze(1).to_broadcast(wide),
                                   ALU.add).then_inc(n_h, 1)
            attention(X, 0)


def kernel(**inputs):
    import numpy as np
    import concourse.bacc as bacc
    from concourse.bass_utils import run_bass_kernel_spmd as run

    a = {k: np.asarray(v) for k, v in inputs.items()}
    t = {k[len("L0_tok_"):]: v for k, v in a.items() if k.startswith("L0_tok_")}
    f = {k[len("L0_ffn_"):]: v for k, v in a.items() if k.startswith("L0_ffn_")}
    cols = [t["ln1_w"], t["ln1_b"]] + [t["qkv_b"][:, k * DIM:(k + 1) * DIM] for k in range(3)]
    cols += [t["ln2_w"], t["ln2_b"], t["fc1_b"][:, 0:DIM], t["fc1_b"][:, DIM:HID]]
    conv = t["conv_w"].reshape(CROWS, 2, PIX, DIM).transpose(1, 0, 2, 3)
    head = (np.arange(P)[:, None] // HD == np.arange(HEADS)[None]).astype(np.float32)
    laid = {
        "x": a["x"].reshape(BATCH * 3, GRID, PATCH, IMG).transpose(0, 2, 1, 3),
        "txt": a["txt"],
        "conv_w": conv,
        "conv_b": t["conv_b"],
        "cls": t["cls_token"].reshape(1, DIM),
        "pos": t["pos_embed"].reshape(NTOK, DIM),
        "qkv_w": t["qkv_w"],
        "proj_w": t["proj_w"],
        "fc1_w": t["fc1_w"],
        "fc2_w": t["fc2_w"],
        "vec": np.stack(cols, axis=2),
        "rows": np.stack([t["proj_b"], t["fc2_b"]], axis=1).reshape(2 * DEPTH, DIM),
        "norm": np.stack([t["norm_w"], t["norm_b"]]),
        "x_w": np.concatenate([a["L0_attn_q_w"], a["L0_attn_kv_w"]]).T,
        "vec_f": np.concatenate([f["ln_g"][:, None], f["ln_b"][:, None],
                                 f["b1"].reshape(EXPERTS * 4, DIM).T], axis=1),
        "w_r": f["w_r"].T,
        "b_r": f["b_r"],
        "w1": f["W1"],
        "w2": f["W2"],
        "b2": f["b2"],
        "c_ident": np.eye(P, dtype=np.float32),
        "c_mask": head,
        "c_sel": (np.arange(P)[:, None] == np.arange(HEADS)[None]).astype(np.float32),
        "c_rank": np.arange(EXPERTS, 0, -1).astype(np.float32),
        "c_eps": np.full((P, 1), EPS, np.float32),
    }
    nc = bacc.Bacc("TRN2", target_bir_lowering=False, num_devices=1)
    arrays, args = {}, {}
    for name, array in laid.items():
        array = np.ascontiguousarray(array)
        arrays[f"in_{name}"] = array
        args[name] = nc.dram_tensor(f"in_{name}", array.shape, mybir.dt.from_np(array.dtype), kind="ExternalInput").ap()
    out = nc.dram_tensor("out_0", (BATCH, NTOK + TXT, DIM), F32, kind="ExternalOutput").ap()
    fusion_kernel(nc, args, out)
    result = run(nc, [arrays], core_ids=[0])
    return result.results[0]["out_0"]
```

```python
from contextlib import ExitStack

import concourse.bass as bass
from concourse import mybir

F32 = mybir.dt.float32
BF16 = mybir.dt.bfloat16
F16 = mybir.dt.float16
ALU = mybir.AluOpType
ACT = mybir.ActivationFunctionType
AX = mybir.AxisListType

P = 128
BATCH = 64
HALF = BATCH // 2
DEPTH = 4
DIM = 128
HEADS = 8
HD = DIM // HEADS
HID = 256
IMG = 224
PATCH = 16
GRID = IMG // PATCH
NPATCH = GRID * GRID
NTOK = NPATCH + 1
TXT = 77
EXPERTS = 8
EHID = 512
EPS = 1e-5
RT = 99
NVIT = 2 * RT
NALL = TXT + NVIT
ROWS = (TXT, RT, RT)
PIX = PATCH // 2
CROWS = 3 * PATCH
SHIFT = 64
GROUP = 32
PAIRS = HEADS // 2
PART = 64
NPAD = 276
VBIAS = 9
SLOTS = 4
IMAGES = 6
PAIRS_PER_PASS = 5
G_EXP = 19
G_ALL = G_EXP + 6
LEAD = 2
WSCALE = 64.0
XSCALE = 16.0
LAG = 2
PIECES = 2 * EXPERTS
STAGES = 4


def need(engine, semaphore, value):
    if not isinstance(value, int) or value > 0:
        engine.wait_ge(semaphore, value)


class Step:

    def __init__(self, i, u):
        if u >= SLOTS:
            i, u = i + 1, u - SLOTS
        elif u < 0:
            i, u = i - 1, u + SLOTS
        self.i, self.u = i, u
        self.n = i * SLOTS + u
        self.k = self.n if isinstance(i, int) else None
        self.sample = i * (SLOTS // 2) + (u // 2 + HALF * (u % 2))

    def at(self, d):
        return Step(self.i, self.u + d)


def job_order(spread):
    order = []
    for m in range(LEAD):
        order += [(name, m) for name in ("T", "Q", "K", "V", *spread)]
    order.append(("M", 0))
    for n in range(BATCH):
        if n + LEAD < BATCH:
            order.append(("T", n + LEAD))
        if n:
            order.append(("E0", n - 1))
        if n + LEAD < BATCH:
            order += [("Q", n + LEAD), ("K", n + LEAD), ("V", n + LEAD)]
        if n:
            order += [("E1", n - 1), ("E2", n - 1)]
        if n + LEAD < BATCH:
            order += [(name, n + LEAD) for name in spread]
        if n + 1 < BATCH:
            order.append(("M", n + 1))
    return order + [("E0", BATCH - 1), ("E1", BATCH - 1), ("E2", BATCH - 1)]


INNER = 5


def bank_of(T, name, s):
    if s.k is not None:
        at = T.jobs[(name, s.k)]
        return at % 2, at // 2
    k = INNER + (s.u - INNER) % SLOTS + SLOTS
    at = T.jobs[(name, k)]
    return at % 2, s.n * (T.per_step // 2) + (at // 2 - k * T.per_step // 2)


class Attention:

    def __init__(self, cross, sem):
        tag = "x_" if cross else "a_"
        self.cross = cross
        self.tiles = ([(0, TXT, TXT, 0), (1, RT, RT, TXT), (2, RT, RT - 1, TXT + RT)] if cross
                      else [(1, RT, RT, 0), (2, RT, RT - 1, RT)])
        self.nq = NALL if cross else NVIT
        self.nk = self.nq - 1
        self.hpu = 1 if cross else 2
        self.upt = HEADS // self.hpu
        self.units = len(self.tiles) * self.upt
        self.slots = [[] for _ in range(8)] + [[2 * w, 2 * w + 1] for w in range(8)] + [[16 + w] for w in range(8)]
        self.even_slots = [[w] for w in range(self.units)]
        if cross:
            self.even_slots, x = [], 0
            for w in range(self.units):
                count = 0 if w < 4 else 2 if w in (10, 12, 14, 16) else 1
                self.even_slots.append(list(range(x, x + count)))
                x += count
        self.cpj = 1 if cross else 2
        self.spread = [f"{side}{c}" for side in "kq" for c in range(PAIRS // self.cpj)]
        self.spread_at = ({w + 6: self.spread[2 * w:2 * w + 2] for w in range(4)} if cross
                          else {6: ["k0", "k1"], 7: ["q0", "q1"]})
        self.act_takes = self.spread[:len(self.spread) // 2] + (self.spread[PAIRS:] if cross else ["q0"])
        self.jobs = {job: at for at, job in enumerate(job_order(self.spread))}
        self.per_step = 8 + len(self.spread)
        self.phase_jobs = len(self.jobs) // 2
        self.tail = 9 if cross else 4
        self.xn_ready = sem(tag + "xn_ready")
        self.job_done = [sem(tag + f"job_done{i}") for i in range(2)]
        self.job_taken = [sem(tag + f"job_taken{i}") for i in range(2)]
        self.hi_ready = sem(tag + "hi_ready")
        self.lo_ready = sem(tag + "lo_ready")
        self.plain_ready = sem(tag + "plain_ready")
        self.max_taken = sem(tag + "max_taken")
        self.score_ready = sem(tag + "score_ready")
        self.exp_ready = sem(tag + "exp_ready")
        self.pv_done = sem(tag + "pv_done")
        self.out_ready = sem(tag + "out_ready")
        self.link = sem(tag + "link")
        self.bias_added = sem(tag + "bias_added")

    def plain_at(self, s, w):
        return (self.slots if self.cross and s.u % 2 else self.even_slots)[w]

    def kv(self, s):
        return s.at(1 if s.u % 2 == 0 else -1) if self.cross else s

    def last_kv(self, s):
        return s.at(1) if self.cross and s.u % 2 == 0 else s


def fusion_kernel(nc, d, out):
    with ExitStack() as ctx:
        def sb(name, shape, dt=F32):
            return ctx.enter_context(nc.sbuf_tensor(name, shape, dt))

        def sem(name):
            return ctx.enter_context(nc.semaphore(name))

        h = sb("h", [P, BATCH * 3 * DIM])
        big = sb("big", [P, 2 * EXPERTS * EHID])
        words = SLOTS * HEADS * NPAD // 2
        qst_words = big[:, 0:words]
        qst = qst_words.bitcast(F16).rearrange("p (s h n) -> p s h n", s=SLOTS, h=HEADS)
        kst = big[:, words:words * 3 // 2].bitcast(F16).rearrange("p (s c n) -> p s c n", s=SLOTS, c=PAIRS)
        qk = big[:, words * 3 // 2:words * 3 // 2 + 4 * NALL].rearrange("p (s k n) -> p s k n", s=2, k=2)
        wparts = big[:, :].bitcast(F16).rearrange("p (w a c n) -> p w a c n", w=PIECES, a=2, c=4)
        att = sb("att", [P, 4 * BATCH * 3 * EXPERTS])
        wconv = att[:, 0:PIX * DIM].rearrange("p (q n) -> p q n", q=PIX)
        posb = att[:, PIX * DIM:PIX * DIM + 2 * DIM].rearrange("p (t n) -> p t n", t=2)
        parts32 = att[:, 2048:2048 + 16 * P]
        imgs = [*(big[:, s * GRID * IMG:(s + 1) * GRID * IMG] for s in range(2)),
                att[:, 4 * BATCH * 3 * EXPERTS - GRID * IMG:]]
        eT = att[:, PIX * DIM + 2 * DIM:PIX * DIM + 2 * DIM + 2 * NVIT].rearrange("p (s n) -> p s n", s=2)
        wqkv = sb("wqkv", [P, 3 * DIM])
        wproj = sb("wproj", [P, DIM])
        wfc1 = sb("wfc1", [P, HID])
        wfc2 = sb("wfc2", [P, 2, DIM])
        vec_a = sb("vec_a", [P, 5])
        vec_m = sb("vec_m", [P, 4])
        row_a = sb("row_a", [P, DIM])
        row_m = sb("row_m", [P, DIM])
        row_v = sb("row_v", [P, P])
        qbias = sb("qbias", [P, 1])
        wx = sb("wx", [P, 3 * DIM])
        norm_rows = sb("norm_rows", [P, 2, DIM])
        vec_f = sb("vec_f", [P, 2 + EXPERTS * 4])
        w_r = sb("w_r", [P, EXPERTS])
        b_r = sb("b_r", [P, EXPERTS])
        br2 = sb("br2", [P, 2 * EXPERTS])
        b2 = sb("b2", [P, DIM])
        ident = sb("ident", [P, P])
        identb = sb("identb", [P, P], BF16)
        parts = sb("parts", [P, 2, 2, PAIRS, P], F16)
        hilo = sb("hilo", [P, 2, 2, 2, NPAD], F16)
        rank = sb("rank", [P, EXPERTS])
        sel32 = sb("sel32", [P, HEADS])
        sel32_e = sb("sel32_e", [P, EXPERTS])
        sel = sb("sel", [P, HEADS, RT], BF16)
        eps = sb("eps", [P, 1])
        xn = sb("xn", [P, 2, 3, DIM])
        yT = sb("yT", [P, 2, NALL])
        vaug = sb("vaug", [P, SLOTS, 3, HEADS, GROUP])
        negm = sb("negm", [P, 2, 3, P], BF16)
        mT = sb("mT", [P, 2, NALL + 1], BF16)
        probs = sb("probs", [P, 4, 2 * NVIT])
        oT = sb("oT", [P, 2, NALL])
        rec = sb("rec", [P, 2, HEADS])
        on = sb("on", [P, 2 * DIM])
        onT = sb("onT", [P, NVIT])
        gT = att[:, 0:4 * NVIT].rearrange("p (s c n) -> p s c n", s=2, c=2)
        bn = sb("bn", [P, 2, 3, 6])
        ag = sb("ag", [P, 2, 3, 2])
        mv = sb("mv", [P, BATCH * 6])
        sd = sb("sd", [P, BATCH * 3])
        rs = sb("rs", [P, BATCH * 3])
        rr = sb("rr", [P, BATCH * 3])
        s1 = sb("s1", [P, BATCH * 3])
        s2 = sb("s2", [P, BATCH * 3])
        NG = BATCH * 3 * EXPERTS
        logit = att[:, 0:NG]
        gate = att[:, NG:2 * NG]
        ga = att[:, 2 * NG:3 * NG]
        gb = att[:, 3 * NG:4 * NG]
        top = probs[:, :, :].rearrange("p s n -> p (s n)")[:, 0:6 * BATCH * 3].rearrange("p (k n) -> p k n", k=6)
        old_v = vaug[:, :, :, :, :].rearrange("p s t h n -> p (s t h n)")
        stage = old_v[:, 0:STAGES * EHID].rearrange("p (s c n) -> p s c n", s=STAGES, c=4)
        hid = old_v[:, 0:8 * NALL].rearrange("p (s c n) -> p s c n", s=2, c=4)
        acc = old_v[:, 8 * NALL:10 * NALL].rearrange("p (s n) -> p s n", s=2)
        hid16 = [words.bitcast(F16).rearrange("p (a c n) -> p a c n", a=2, c=4)
                 for words in (ga[:, 0:4 * NALL], att[:, 2 * NG + 4 * NALL:2 * NG + 8 * NALL], logit[:, 0:4 * NALL],
                               probs[:, :, :].rearrange("p s n -> p (s n)")[:, 0:4 * NALL])]
        old_parts = parts[:, :, :, :, :].rearrange("p a b c n -> p (a b c n)")
        gsel = old_parts[:, 0:EXPERTS * P].rearrange("p (e n) -> p e n", e=EXPERTS)
        part_out = old_parts[:, EXPERTS * P:2 * EXPERTS * P].bitcast(F32)[:, 0:NALL]
        y16 = hilo[:, :, :, 0, :]
        gate16 = hilo[:, :, 0, 1, :]
        gates = att[:, 2 * NG + 8 * NALL:2 * NG + 10 * NALL].rearrange("p (s n) -> p s n", s=2)
        vec_y = sb("vec_y", [P, 2])
        gnow = wqkv[:, :].rearrange("p (t n) -> p t n", t=3)
        gateT = oT[0:EXPERTS, :, :]

        misc = [ctx.enter_context(nc.psum_tensor(f"misc{i}", [P, 512], F32)) for i in range(2)]
        plain = [ctx.enter_context(nc.psum_tensor(f"plain{i}", [P, 512], F32)) for i in range(2)]
        score = [ctx.enter_context(nc.psum_tensor(f"score{i}", [P, 512], F32)) for i in range(2)]
        outp = [ctx.enter_context(nc.psum_tensor(f"outp{i}", [P, 512], F32)) for i in range(2)]

        const_in = sem("const_in")
        txt_in = sem("txt_in")
        setup_v = sem("setup_v")
        img_in = [sem(f"img_in{i}") for i in range(3)]
        parts_v = sem("parts_v")
        conv_done = sem("conv_done")
        conv_taken = sem("conv_taken")
        emb_done = sem("emb_done")
        emb_link = sem("emb_link")
        wa_in = sem("wa_in")
        wm_in = sem("wm_in")
        moe_in = [sem(f"moe_in{i}") for i in range(STAGES)]
        sd_ready = sem("sd_ready")
        rs_ready = sem("rs_ready")
        fold_v = sem("fold_v")
        fold_pe = sem("fold_pe")
        fold_done = sem("fold_done")
        m_xn = sem("m_xn")
        m_t = sem("m_t")
        m_y = sem("m_y")
        m_f1 = sem("m_f1")
        m_g = sem("m_g")
        m_f2 = sem("m_f2")
        m_bias = sem("m_bias")
        m_link = sem("m_link")
        n_xn = sem("n_xn")
        n_w = sem("n_w")
        n_h = sem("n_h")
        n_link = sem("n_link")
        r_xn = sem("r_xn")
        r_t = sem("r_t")
        r_y = sem("r_y")
        r_l = sem("r_l")
        r_done = sem("r_done")
        g_v = sem("g_v")
        g_exp = sem("g_exp")
        split_hi = sem("split_hi")
        split_p = sem("split_p")
        e_const = sem("e_const")
        e_xn = sem("e_xn")
        e_t = sem("e_t")
        e_y = sem("e_y")
        e_yhi = sem("e_yhi")
        e_ylo = sem("e_ylo")
        e_gn = sem("e_gn")
        e_gt = sem("e_gt")
        e_gs = sem("e_gs")
        e_b2 = sem("e_b2")
        e_b2t = sem("e_b2t")
        e_f1 = sem("e_f1")
        e_g = sem("e_g")
        e_hi = sem("e_hi")
        e_lo = sem("e_lo")
        e_gb = sem("e_gb")
        e_gc = sem("e_gc")
        e_f2 = sem("e_f2")
        e_part = sem("e_part")
        e_acc = sem("e_acc")
        e_s = sem("e_s")
        e_back = sem("e_back")
        e_h = sem("e_h")
        out_done = sem("out_done")
        passed_v = sem("passed_v")
        passed_p = sem("passed_p")
        A = Attention(False, sem)
        X = Attention(True, sem)

        def h_tile(b, t, rows=None):
            return h[0:ROWS[t] if rows is None else rows, bass.ds(b * (3 * DIM) + t * DIM, DIM)]

        def h_image(b):
            return h[0:RT, bass.ds(b * (3 * DIM) + DIM, 2 * DIM)]

        def stat(array, b, t):
            return array[0:ROWS[t], bass.ds(b * 3 + t, 1)]

        def mean(b, t):
            return mv[0:ROWS[t], bass.ds(b * 6 + 2 * t, 1)]

        QUEUED = 2
        CONSTS = 20
        WA, WM = 4, 4

        block = ctx.enter_context(nc.Block())

        @block.sync
        def _(sp):
            def const(dst, src):
                sp.dma_start(dst, src).then_inc(const_in, 16)

            sp.wait_ge(setup_v, 1)
            with nc.allow_non_contiguous_dma(reason="small rows of constants"):
                const(ident[:, :], d["c_ident"])
                const(parts32, d["c_parts"])
                const(rank[:, :], d["c_rank"].partition_broadcast(P))
                const(sel32[:, :], d["c_sel"])
                const(sel32_e[:, :], d["c_sel_e"])
                for half in range(2):
                    const(wconv[half * SHIFT:half * SHIFT + CROWS, :, :], d["conv_w"][half])
                const(on[0:RT, 0:DIM], d["pos"][0:RT, :])
                const(on[0:RT - 1, DIM:2 * DIM], d["pos"][RT:NTOK, :])
                const(probs[1:RT, 0, 0:DIM], d["conv_b"].partition_broadcast(RT - 1))
                const(probs[0:RT, 0, DIM:2 * DIM], d["conv_b"].partition_broadcast(RT))
                const(probs[0:1, 0, 0:DIM], d["cls"])
                const(wx[:, :], d["x_w"])
                for t in range(2):
                    const(norm_rows[0:RT, t, :], d["norm"][t].partition_broadcast(RT))
                const(vec_f[:, :], d["vec_f"])
                const(w_r[:, :], d["w_r"])
                const(b_r[0:RT, :], d["b_r"].partition_broadcast(RT))
                const(b2[0:EXPERTS, :], d["b2"])
                const(eps[:, :], d["c_eps"])
            sp.dma_start(h[0:TXT, :].rearrange("p (b t n) -> p b t n", b=BATCH, t=3)[:, :, 0, :],
                         d["txt"].rearrange("b p n -> p b n")).then_inc(txt_in, 16)

            def load_image(b, slot):
                img = imgs[slot].rearrange("p (g w) -> p g w", g=GRID)
                for half in range(2):
                    lo = half * SHIFT
                    sp.dma_start(img[lo:lo + CROWS, :, 0:IMG - half * PIX],
                                 d["x"][bass.ds(b * 3, 3), :, :, half * PIX:IMG]
                                 .rearrange("c p g w -> (c p) g w")).then_inc(img_in[slot], 16)

            sp.wait_ge(parts_v, 2)
            for b in range(3):
                load_image(b, b)
            with sp.Fori(0, (BATCH - 4) // IMAGES) as i:
                for k in range(IMAGES):
                    b = i * IMAGES + (k + 3)
                    sp.wait_ge(conv_done, b - 2)
                    load_image(b, k % 3)
            sp.wait_ge(conv_done, BATCH - 3)
            load_image(BATCH - 1, (BATCH - 1) % 3)

            def load_attention(l):
                sp.dma_start(wqkv[:, :], d["qkv_w"][bass.ds(l, 1)].rearrange("o k n -> (o k) n")).then_inc(wa_in, 16)
                sp.dma_start(wproj[:, :], d["proj_w"][bass.ds(l, 1)].rearrange("o k n -> (o k) n")).then_inc(wa_in, 16)
                sp.dma_start(vec_a[:, :], d["vec"][bass.ds(l, 1), :, 0:5].rearrange("o k n -> (o k) n")).then_inc(wa_in, 16)
                sp.dma_start(row_a[0:RT, :], d["rows"][bass.ds(l * 2, 1), :].broadcast_to([RT, DIM])).then_inc(wa_in, 16)

            def load_mlp(l):
                sp.dma_start(wfc1[:, :], d["fc1_w"][bass.ds(l, 1)].rearrange("o k n -> (o k) n")).then_inc(wm_in, 16)
                sp.dma_start(wfc2[:, :, :], d["fc2_w"][bass.ds(l, 1)].rearrange("o (c k) n -> (o k) c n", c=2)).then_inc(wm_in, 16)
                sp.dma_start(vec_m[:, :], d["vec"][bass.ds(l, 1), :, 5:VBIAS].rearrange("o k n -> (o k) n")).then_inc(wm_in, 16)
                sp.dma_start(row_m[0:RT, :], d["rows"][bass.ds(l * 2 + 1, 1), :].broadcast_to([RT, DIM])).then_inc(wm_in, 16)

            with nc.allow_non_contiguous_dma(reason="small rows of constants"):
                load_attention(0)
                load_mlp(0)
                with sp.Fori(1, DEPTH) as l:
                    sp.wait_ge(A.link, l * (A.tail * BATCH))
                    load_attention(l)
                    sp.wait_ge(m_link, l * (4 * BATCH))
                    load_mlp(l)
            sp.wait_ge(X.link, X.tail * BATCH)
            for w in range(PIECES):
                if w >= STAGES:
                    sp.wait_ge(split_p, w - STAGES + 1)
                e, which = w // 2, w % 2
                src = d["w2"][e].rearrange("(c k) n -> k c n", c=4) if which else d["w1"][e].rearrange("k (c n) -> k c n", c=4)
                sp.dma_start(stage[:, w % STAGES, :, :], src).then_inc(moe_in[w % STAGES], 16)
            with sp.Fori(0, BATCH) as b:
                sp.wait_ge(e_h, b + 1)
                for t, lo, rows in ((0, NTOK, TXT), (1, 0, RT), (2, RT, RT - 1)):
                    sp.dma_start(out[bass.ds(b, 1), lo:lo + rows, :].rearrange("o p n -> (o p) n"),
                                 h_tile(b, t, rows)).then_inc(out_done, 16)
            sp.wait_ge(out_done, 16 * 3 * BATCH)

        @block.tensor
        def _(pe):
            pe.wait_ge(const_in, 16 * CONSTS)
            pe.wait_ge(setup_v, 2)

            def conv(b, u, slot, loads, first=False):
                pe.wait_ge(img_in[slot], loads * (16 * QUEUED))
                if not first:
                    pe.wait_ge(conv_taken, b - 1)
                img = imgs[slot].rearrange("p (g x q) -> p g x q", g=GRID, q=PATCH)
                for q in range(PIX):
                    mm = pe.matmul(misc[u][:, 0:NPATCH], wconv[0:SHIFT + CROWS, q, :],
                                   img[0:SHIFT + CROWS, :, :, q], start=(q == 0), stop=(q == PIX - 1))
                mm.then_inc(conv_done, 1)

            def embed(b, u, first=False):
                pe.wait_ge(conv_taken, b + 1)
                if not first:
                    pe.wait_ge(emb_link, b * 4 - 7)
                for t in range(2):
                    mm = pe.transpose(plain[u][0:RT, t * DIM:(t + 1) * DIM],
                                      eT[:, u, t * RT:(t + 1) * RT], ident[:, :])
                mm.then_inc(emb_done, 1)

            for b in range(2):
                conv(b, b, b, 1, True)
            for b in range(2):
                embed(b, b, True)
            with pe.Fori(0, (BATCH - 4) // IMAGES) as i:
                for k in range(0, IMAGES, 2):
                    for u in range(2):
                        conv(i * IMAGES + (k + u + 2), u, (k + u + 2) % 3, i * (IMAGES // 3) + ((k + u + 2) // 3 + 1))
                    for u in range(2):
                        embed(i * IMAGES + (k + u + 2), u)
            for b in range(BATCH - 2, BATCH):
                conv(b, b % 2, b % 3, b // 3 + 1)
            for b in range(BATCH - 2, BATCH):
                embed(b, b % 2)

            def project(T, s, base, names, wq, wk, wv):
                y = yT[:, s.u % 2, :]
                for name in names:
                    bank, at = bank_of(T, name, s)
                    pe.wait_ge(T.job_taken[bank], base * T.phase_jobs + (at + 1))
                    if name == "T":
                        pe.wait_ge(T.xn_ready, base * BATCH + s.n + 1)
                        for t, (_, rows, _, col) in enumerate(T.tiles):
                            mm = pe.transpose(misc[bank][:, col:col + rows], xn[0:rows, s.u % 2, t, :],
                                              ident[0:rows, 0:rows])
                    elif name == "V":
                        for t, (_, rows, _, col) in enumerate(T.tiles):
                            mm = pe.matmul(misc[bank][0:rows, t * DIM:(t + 1) * DIM], y[:, col:col + rows], wv,
                                           start=True, stop=True)
                    else:
                        if name == "Q":
                            tbank, tat = bank_of(T, "T", s)
                            pe.wait_ge(T.job_taken[tbank], base * T.phase_jobs + (tat + 2))
                        mm = pe.matmul(misc[bank][:, 0:T.nq], wq if name == "Q" else wk, y[:, 0:T.nq],
                                       start=True, stop=True)
                    mm.then_inc(T.job_done[bank], 1)

            def spread(T, s, base, name):
                bank, at = bank_of(T, name, s)
                pe.wait_ge(T.job_taken[bank], base * T.phase_jobs + (at + 1))
                pe.wait_ge(T.lo_ready, base * BATCH + s.n + 1)
                side = "qk".index(name[0])
                for j in range(T.cpj):
                    for part in range(2):
                        mm = pe.matmul(misc[bank][:, j * T.nq:(j + 1) * T.nq],
                                       parts[:, side, part, int(name[1]) * T.cpj + j, :],
                                       hilo[:, s.u % 2, part, side, 0:T.nq], start=(part == 0), stop=(part == 1))
                mm.then_inc(T.job_done[bank], 1)

            def spread_taken(T, s, base, names):
                for name in names:
                    bank, at = bank_of(T, name, s if name[0] == "q" else T.last_kv(s))
                    pe.wait_ge(T.job_taken[bank], base * T.phase_jobs + (at + 2))

            def plain_unit(T, s, base, w):
                if w == 0:
                    spread_taken(T, s, base, [side + str(PAIRS // T.cpj - 1) for side in "kq"])
                if not (s.k == 0 and w < 2):
                    pe.wait_ge(T.max_taken, (base * BATCH + s.n) * T.units + (w - 1))
                _, rows, _, col = T.tiles[w // T.upt]
                for j in range(T.hpu):
                    hd = (w % T.upt) * T.hpu + j
                    mm = pe.matmul(plain[w % 2][0:rows, j * 256:j * 256 + T.nk], qst[:, s.u, hd, col:col + rows],
                                   kst[:, T.kv(s).u, hd // 2, 0:T.nk], start=True, stop=True)
                mm.then_inc(T.plain_ready, 1)

            def max_job(T, s, base):
                bank, at = bank_of(T, "M", s)
                pe.wait_ge(T.job_taken[bank], base * T.phase_jobs + (at + 1))
                pe.wait_ge(T.max_taken, (base * BATCH + s.n + 1) * T.units)
                low = misc[bank][:, :].bitcast(BF16)
                for t, (_, rows, _, col) in enumerate(T.tiles):
                    mm = pe.transpose(low[:, t * P:t * P + rows], negm[0:rows, s.u % 2, t, :],
                                      identb[0:rows, 0:rows])
                mm.then_inc(T.job_done[bank], 1)

            def score_unit(T, s, base, w):
                if w == 0:
                    spread_taken(T, s, base, [side + str(PAIRS // T.cpj - 1) for side in "kq"])
                    bank, at = bank_of(T, "M", s)
                    pe.wait_ge(T.job_taken[bank], base * T.phase_jobs + (at + 2))
                if not (s.k == 0 and w < 2):
                    pe.wait_ge(T.exp_ready, (base * BATCH + s.n) * T.units + (w - 1))
                _, _, rows, col = T.tiles[w // T.upt]
                h0 = (w % T.upt) * T.hpu
                pe.matmul(score[w % 2][0:rows, 0:T.hpu * T.nq], kst[:, T.kv(s).u, h0 // 2, col:col + rows],
                          qst[:, s.u, h0:h0 + T.hpu, 0:T.nq], start=True, stop=False)
                for j in range(T.hpu):
                    mm = pe.matmul(score[w % 2][0:rows, j * T.nq:(j + 1) * T.nq], sel[:, h0 + j, 0:rows],
                                   mT[:, s.u % 2, 0:T.nq], start=False, stop=(j == T.hpu - 1))
                mm.then_inc(T.score_ready, 1)

            def value_unit(T, s, base, w):
                if w == 0:
                    bank, at = bank_of(T, "V", T.kv(s))
                    pe.wait_ge(T.job_taken[bank], base * T.phase_jobs + (at + 2))
                    pe.wait_ge(T.out_ready, base * BATCH + (s.n + 1))
                pe.wait_ge(T.exp_ready, (base * BATCH + s.n) * T.units + (w + 1))
                t = w // T.upt
                rows = T.tiles[t][2]
                for j in range(T.hpu):
                    hd = (w % T.upt) * T.hpu + j
                    lo = GROUP * (hd % 4)
                    mm = pe.matmul(outp[hd // 4][lo:lo + GROUP, 0:T.nq], vaug[0:rows, T.kv(s).u, t, hd, :],
                                   probs[0:rows, w % 4, j * T.nq:(j + 1) * T.nq],
                                   start=(t == 0), stop=(t == len(T.tiles) - 1), tile_position=(0, lo))
                mm.then_inc(T.pv_done, 1)

            def back(T, s, base, tiles, name):
                bank, at = bank_of(T, name, s)
                pe.wait_ge(T.job_taken[bank], base * T.phase_jobs + (at + 1))
                pe.wait_ge(T.out_ready, base * BATCH + (s.n + 2))
                for k, t in enumerate(tiles):
                    _, rows, _, col = T.tiles[t]
                    for c in range(2):
                        mm = pe.transpose(misc[bank][0:rows, (2 * k + c) * P:(2 * k + c + 1) * P],
                                          oT[:, c, col:col + rows], ident[:, :])
                mm.then_inc(T.job_done[bank], 1)

            def end_job(T, s, base, j):
                name = f"E{j}"
                if T.cross:
                    back(T, s, base, [j], name)
                    return
                if j == 0:
                    back(T, s, base, [0, 1], name)
                    return
                bank, at = bank_of(T, name, s)
                pe.wait_ge(T.job_taken[bank], base * T.phase_jobs + (at + 1))
                pbank, pat = bank_of(T, f"E{j - 1}", s)
                pe.wait_ge(T.job_taken[pbank], base * T.phase_jobs + (pat + 2))
                for t in range(2):
                    if j == 1:
                        mm = pe.transpose(misc[bank][:, t * RT:(t + 1) * RT], on[0:RT, t * DIM:(t + 1) * DIM],
                                          ident[0:RT, 0:RT])
                    else:
                        mm = pe.matmul(misc[bank][0:RT, t * DIM:(t + 1) * DIM], onT[:, t * RT:(t + 1) * RT],
                                       wproj[:, :], start=True, stop=True)
                mm.then_inc(T.job_done[bank], 1)

            def attention(T, base, w_all):
                wq, wk, wv = (w_all[:, k * DIM:(k + 1) * DIM] for k in range(3))
                for m in range(LEAD):
                    project(T, Step(0, m), base, "TQKV", wq, wk, wv)
                    for name in T.spread:
                        spread(T, Step(0, m), base, name)
                for w in range(T.units):
                    plain_unit(T, Step(0, 0), base, w)
                max_job(T, Step(0, 0), base)

                def step(s):
                    ahead = s.k is None or s.k + LEAD < BATCH
                    more = s.k is None or s.k + 1 < BATCH
                    for w in range(T.units):
                        if w == 1 and s.k != 0:
                            end_job(T, s.at(-1), base, 0)
                        if w == 2 and ahead:
                            project(T, s.at(LEAD), base, "QK", wq, wk, wv)
                        if w == 3 and s.k != 0:
                            end_job(T, s.at(-1), base, 1)
                        if w == 5 and s.k != 0:
                            end_job(T, s.at(-1), base, 2)
                        early = not T.cross and w == T.units - 1
                        for k, name in enumerate(T.spread_at.get(w, ())):
                            if ahead:
                                spread(T, s.at(LEAD), base, name)
                            if early and more and k == 0:
                                plain_unit(T, s.at(1), base, w)
                        if w == 0 and ahead and T.cross:
                            project(T, s.at(LEAD), base, "T", wq, wk, wv)
                        score_unit(T, s, base, w)
                        if w == 0 and ahead and not T.cross:
                            project(T, s.at(LEAD), base, "T", wq, wk, wv)
                        if w == 2 and ahead:
                            project(T, s.at(LEAD), base, "V", wq, wk, wv)
                        if w >= 2:
                            value_unit(T, s, base, w - 2)
                        if more and not early:
                            for x in T.plain_at(s, w):
                                plain_unit(T, s.at(1), base, x)
                    value_unit(T, s, base, T.units - 2)
                    if more:
                        max_job(T, s.at(1), base)
                    value_unit(T, s, base, T.units - 1)

                for u in range(SLOTS):
                    step(Step(0, u))
                with pe.Fori(0, (BATCH // SLOTS - 2) // 2) as i:
                    for u in range(2 * SLOTS):
                        step(Step(i * 2 + 1, u))
                for u in range(SLOTS):
                    step(Step(BATCH // SLOTS - 1, u))
                for j in range(3):
                    end_job(T, Step(BATCH // SLOTS - 1, SLOTS - 1), base, j)

            def mlp(l):
                def turn(n, u):
                    pe.wait_ge(m_xn, l * BATCH + n + 1)
                    if isinstance(n, int):
                        if n > 1:
                            pe.wait_ge(m_y, l * BATCH + n - 1)
                    else:
                        pe.wait_ge(m_y, l * BATCH + n - 1)
                    for t in range(2):
                        mm = pe.transpose(misc[u][:, t * RT:(t + 1) * RT], xn[0:RT, u, t, :], ident[0:RT, 0:RT])
                    mm.then_inc(m_t, 1)

                def fc1(n, u, first=False):
                    pe.wait_ge(m_y, l * BATCH + n + 1)
                    if not first:
                        pe.wait_ge(m_g, l * BATCH + n - 1)
                    for c in range(2):
                        mm = pe.matmul(plain[u][:, c * NVIT:(c + 1) * NVIT], wfc1[:, c * P:(c + 1) * P],
                                       yT[:, u, 0:NVIT], start=True, stop=True)
                    mm.then_inc(m_f1, 1)

                def fc2(n, u, first=False):
                    pe.wait_ge(m_g, l * BATCH + n + 1)
                    if not first:
                        pe.wait_ge(m_link, (l * BATCH + n) * 4 - (7 + 2 * u))
                    for t in range(2):
                        for c in range(2):
                            mm = pe.matmul(score[u][0:RT, t * DIM:(t + 1) * DIM], gT[:, u, c, t * RT:(t + 1) * RT],
                                           wfc2[:, c, :], start=(c == 0), stop=(c == 1))
                    mm.then_inc(m_f2, 1)

                turn(0, 0)
                turn(1, 1)
                fc1(0, 0, True)
                for n in range(2):
                    turn(n + 2, n)
                    fc1(n + 1, (n + 1) % 2, n == 0)
                    fc2(n, n, True)
                with pe.Fori(0, (HALF - 2) // PAIRS_PER_PASS) as i:
                    for k in range(2 * PAIRS_PER_PASS):
                        n = i * (2 * PAIRS_PER_PASS) + (k + 2)
                        turn(n + 2, k % 2)
                        fc1(n + 1, (k + 1) % 2)
                        fc2(n, k % 2)
                fc1(BATCH - 1, 1)
                fc2(BATCH - 2, 0)
                fc2(BATCH - 1, 1)

            with pe.Fori(0, DEPTH) as l:
                pe.wait_ge(wa_in, l * (16 * WA) + 16 * WA)
                pe.wait_ge(fold_v, l + 1)
                pe.matmul(plain[0][0:RT, 0:DIM], row_v[:, 0:RT], wproj[:, :], start=True, stop=True).then_inc(fold_pe, 1)
                pe.wait_ge(fold_done, l + 1)
                attention(A, l, wqkv)
                pe.wait_ge(wm_in, l * (16 * WM) + 16 * WM)
                mlp(l)
            attention(X, 0, wx)

            def turn_all(bank, slot, done):
                for t, (_, rows, _, col) in enumerate(X.tiles):
                    mm = pe.transpose(misc[bank][:, col:col + rows], xn[0:rows, slot, t, :], ident[0:rows, 0:rows])
                mm.then_inc(done, 1)

            def router_turn(n, u, first=False):
                pe.wait_ge(r_xn, n + 1)
                if not first:
                    pe.wait_ge(r_y, n - 1)
                turn_all(u, u, r_t)

            def router(n, u, first=False):
                pe.wait_ge(r_y, n + 1)
                if not first:
                    pe.wait_ge(r_done, n - 1)
                for t, (_, rows, _, col) in enumerate(X.tiles):
                    mm = pe.matmul(plain[u][0:rows, t * EXPERTS:(t + 1) * EXPERTS], yT[:, u, col:col + rows],
                                   w_r[:, :], start=True, stop=True)
                mm.then_inc(r_l, 1)

            router_turn(0, 0, True)
            router_turn(1, 1, True)
            router(0, 0, True)
            router_turn(2, 0)
            router(1, 1, True)
            with pe.Fori(0, (HALF - 2) // PAIRS_PER_PASS) as i:
                for k in range(2 * PAIRS_PER_PASS):
                    n = i * (2 * PAIRS_PER_PASS) + (k + 2)
                    router_turn(n + 1, (k + 1) % 2)
                    router(n, k % 2)
            router_turn(BATCH - 1, 1)
            router(BATCH - 2, 0)
            router(BATCH - 1, 1)

            PASSES = ((0, 0), (0, 1), (1, 0))

            def expert_turn(n, u):
                pe.wait_ge(e_xn, n + 1)
                need(pe, e_h, n - 1)
                turn_all(0, u, e_t)

            def turn_gates(n):
                pe.wait_ge(e_gn, n + 1)
                pe.wait_ge(e_y, n + 1)
                for t, (_, rows, _, col) in enumerate(X.tiles):
                    mm = pe.transpose(misc[0][:, col:col + rows], gnow[0:rows, t, :],
                                      ident[0:rows, 0:rows])
                mm.then_inc(e_gt, 1)

            def output_bias(n, u):
                pe.wait_ge(e_gs, n * 3 + 3)
                pe.matmul(misc[0][:, 0:NALL], b2[0:EXPERTS, :], gateT[:, u, 0:NALL],
                          start=True, stop=True).then_inc(e_b2, 1)

            def fc1_chunk(n, u, e, c):
                need(pe, e_g, (n * 8 + e) * 4 + (c - 3))
                bank = (plain + score)[c]
                for k, (w, y) in enumerate(PASSES):
                    mm = pe.matmul(bank[:, 0:NALL], wparts[:, 2 * e, w, c, :], y16[:, u, y, 0:NALL],
                                   start=(k == 0), stop=(k == 2))
                mm.then_inc(e_f1, 1)

            def fc2_expert(n, u, e):
                g = n * 8 + e
                need(pe, e_gc, g)
                pe.matmul(misc[1][:, 0:NALL], gsel[:, e, :], gate16[:, u, 0:NALL],
                          start=True, stop=True).then_inc(e_gb, 1)
                pe.wait_ge(e_lo, g * 2 + 2)
                need(pe, e_part, g - 1)
                for c in range(4):
                    for k, (w, y) in enumerate(PASSES):
                        mm = pe.matmul(outp[e % 2][:, 0:NALL], wparts[:, 2 * e + 1, w, c, :],
                                       hid16[e % 4][:, y, c, :], start=(c == 0 and k == 0), stop=(c == 3 and k == 2))
                mm.then_inc(e_f2, 1)

            def turn_back(n, u):
                pe.wait_ge(e_acc, n * 8 + 8)
                for t, (_, rows, _, col) in enumerate(X.tiles):
                    mm = pe.transpose(misc[0][0:rows, t * DIM:(t + 1) * DIM], acc[:, u, col:col + rows], ident[:, :])
                mm.then_inc(e_back, 1)

            def experts(n, u, first=False, last=False):
                pe.wait_ge(e_ylo, n + 1)
                for e in range(EXPERTS):
                    for c in range(4):
                        fc1_chunk(n, u, e, c)
                    if e == 2 and not first:
                        pe.wait_ge(e_b2t, n + 1)
                        turn_back(n - 1, 1 - u)
                    if e == 7 and not last:
                        output_bias(n + 1, 1 - u)
                    if e >= LAG:
                        fc2_expert(n, u, e - LAG)
                    elif not first:
                        fc2_expert(n - 1, 1 - u, e - LAG + EXPERTS)
                    if e == 3 and not last:
                        expert_turn(n + 1, 1 - u)
                    if e == 4 and not last:
                        turn_gates(n + 1)

            pe.wait_ge(split_p, PIECES)
            pe.wait_ge(e_const, 2)
            expert_turn(0, 0)
            turn_gates(0)
            output_bias(0, 0)
            experts(0, 0, first=True)
            experts(1, 1)
            with pe.Fori(1, HALF - 1) as i:
                for u in range(2):
                    experts(i * 2 + u, u)
            experts(BATCH - 2, 0)
            experts(BATCH - 1, 1, last=True)
            for e in range(EXPERTS - LAG, EXPERTS):
                fc2_expert(BATCH - 1, 1, e)
            turn_back(BATCH - 1, 1)

        @block.scalar
        def _(act):
            act.wait_ge(const_in, 16 * CONSTS)
            act.wait_ge(setup_v, 2)
            with act.Fori(0, HALF) as i:
                for u in range(2):
                    act.wait_ge(conv_done, i * 2 + (u + 1))
                    act.activation(eT[:, u, 1:1 + NPATCH], misc[u][:, 0:NPATCH], ACT.Copy).then_inc(conv_taken, 1)

            def deviation(src):
                act.activation(sd[0:RT, :], src, ACT.Sqrt, bias=eps[0:RT, :]).then_inc(sd_ready, 1)

            variances = mv[0:RT, :].rearrange("p (n s) -> p n s", s=2)[:, :, 1]

            def take(T, s, base, name):
                bank, at = bank_of(T, name, s)
                act.wait_ge(T.job_done[bank], base * T.phase_jobs + (at + 1))
                return misc[bank], T.job_taken[bank]

            def take_turned(T, s, base):
                ps, taken = take(T, s, base, "T")
                y = yT[:, s.u % 2, 0:T.nq]
                if T.cross:
                    act.activation(y, ps[:, 0:T.nq], ACT.Copy).then_inc(taken, 1)
                else:
                    act.activation(y, ps[:, 0:T.nq], ACT.Identity, bias=vec_a[:, 1:2],
                                   scale=vec_a[:, 0:1]).then_inc(taken, 1)

            def take_projection(T, s, base, used):
                if used:
                    act.wait_ge(T.lo_ready, base * BATCH + s.n - 1)
                for k, name in enumerate("QK"):
                    ps, taken = take(T, s, base, name)
                    dst = qk[:, s.u % 2, k, 0:T.nq]
                    if T.cross:
                        ins = act.activation(dst, ps[:, 0:T.nq], ACT.Copy, scale=1.0 if k else float(DIM) ** -0.5)
                    elif k:
                        ins = act.activation(dst, ps[:, 0:T.nq], ACT.Identity, bias=vec_a[:, 3:4])
                    else:
                        ins = act.activation(dst, ps[:, 0:T.nq], ACT.Identity, bias=qbias[:, :],
                                             scale=float(HD) ** -0.5)
                    ins.then_inc(taken, 1)

            def take_spread(T, s, base, name):
                ps, taken = take(T, s, base, name)
                c = int(name[1]) * T.cpj
                if name[0] == "q":
                    block = ps[:, 0:T.cpj * T.nq].rearrange("p (c n) -> p c n", c=T.cpj)
                    for half in range(2):
                        h0 = 2 * c + half
                        ins = act.activation(qst[half * PART:(half + 1) * PART, s.u, h0:h0 + 2 * T.cpj - 1:2, 0:T.nq],
                                             block[half * PART:(half + 1) * PART, :, :], ACT.Copy)
                    ins.then_inc(taken, 1)
                    return
                act.activation(kst[:, s.u, c:c + T.cpj, 0:T.nq],
                               ps[:, 0:T.cpj * T.nq].rearrange("p (c n) -> p c n", c=T.cpj),
                               ACT.Copy).then_inc(taken, 1)

            def take_value(T, s, base):
                ps, taken = take(T, s, base, "V")
                v = ps[:, 0:len(T.tiles) * DIM].rearrange("p (t h d) -> p t h d", t=len(T.tiles), h=HEADS)
                first = 0
                if T.cross:
                    act.activation(vaug[0:TXT, s.u, 0, :, 0:HD], v[0:TXT, 0], ACT.Copy)
                    first = 1
                act.activation(vaug[0:RT, s.u, first:first + 2, :, 0:HD], v[0:RT, first:first + 2],
                               ACT.Copy).then_inc(taken, 1)

            def take_max(T, s, base):
                ps, taken = take(T, s, base, "M")
                low = ps[:, :].bitcast(BF16)
                first, col = 0, 0
                if T.cross:
                    act.activation(mT[:, s.u % 2, 0:TXT], low[:, 0:TXT], ACT.Copy)
                    first, col = 1, TXT
                act.activation(mT[:, s.u % 2, col:col + 2 * RT].rearrange("p (t n) -> p t n", t=2),
                               low[:, first * P:(first + 2) * P].rearrange("p (t n) -> p t n", t=2)[:, :, 0:RT],
                               ACT.Copy).then_inc(taken, 1)

            def take_output(T, s, base):
                act.wait_ge(T.pv_done, (base * BATCH + (s.n + 1)) * T.units)
                for c in range(2):
                    ins = act.activation(oT[:, c, 0:T.nq], outp[c][:, 0:T.nq], ACT.Copy)
                ins.then_inc(T.out_ready, 1)

            def exp_unit(T, s, base, w):
                act.wait_ge(T.score_ready, (base * BATCH + s.n) * T.units + (w + 1))
                if not (s.k == 0 and w < 4):
                    act.wait_ge(T.pv_done, (base * BATCH + s.n) * T.units + (w - 3))
                rows = T.tiles[w // T.upt][2]
                act.activation(probs[0:rows, w % 4, 0:T.hpu * T.nq], score[w % 2][0:rows, 0:T.hpu * T.nq],
                               ACT.Exp).then_inc(T.exp_ready, 1)

            def attention(T, base):
                for m in range(LEAD):
                    take_turned(T, Step(0, m), base)
                    take_projection(T, Step(0, m), base, False)
                    take_value(T, Step(0, m), base)
                    for name in T.act_takes:
                        take_spread(T, Step(0, m), base, name)
                take_max(T, Step(0, 0), base)

                def step(s):
                    ahead = s.k is None or s.k + LEAD < BATCH
                    for w in range(T.units):
                        if w == 2 and ahead:
                            take_projection(T, s.at(LEAD), base, True)
                        if w == 3 and s.k != 0 and not T.cross:
                            take_heads(T, s.at(-1), base)
                        if ahead:
                            for name in T.spread_at.get(w, ()):
                                if name in T.act_takes:
                                    take_spread(T, s.at(LEAD), base, name)
                        if w == 0 and ahead and T.cross:
                            take_turned(T, s.at(LEAD), base)
                        exp_unit(T, s, base, w)
                        if w == 0 and ahead and not T.cross:
                            take_turned(T, s.at(LEAD), base)
                        if w == 2 and ahead:
                            take_value(T, s.at(LEAD), base)
                    if s.k is None or s.k + 1 < BATCH:
                        take_max(T, s.at(1), base)
                    take_output(T, s, base)

                def take_heads(T, s, base):
                    ps, taken = take(T, s, base, "E1")
                    act.activation(onT[:, :], ps[:, 0:NVIT], ACT.Copy).then_inc(taken, 1)

                for u in range(SLOTS):
                    step(Step(0, u))
                with act.Fori(0, (BATCH // SLOTS - 2) // 2) as i:
                    for u in range(2 * SLOTS):
                        step(Step(i * 2 + 1, u))
                for u in range(SLOTS):
                    step(Step(BATCH // SLOTS - 1, u))
                if not T.cross:
                    take_heads(T, Step(BATCH // SLOTS - 1, SLOTS - 1), base)

            def mlp(l):
                def norm(n, u):
                    act.wait_ge(m_t, l * BATCH + n + 1)
                    act.activation(yT[:, u, 0:NVIT], misc[u][:, 0:NVIT], ACT.Identity, bias=vec_m[:, 1:2],
                                   scale=vec_m[:, 0:1]).then_inc(m_y, 1)

                def gelu(n, u):
                    act.wait_ge(m_f1, l * BATCH + n + 1)
                    for c in range(2):
                        ins = act.activation(gT[:, u, c, :], plain[u][:, c * NVIT:(c + 1) * NVIT], ACT.Gelu,
                                             bias=vec_m[:, 2 + c:3 + c])
                    ins.then_inc(m_g, 1)

                norm(0, 0)
                norm(1, 1)
                gelu(0, 0)
                with act.Fori(0, HALF - 1) as i:
                    for u in range(2):
                        norm(i * 2 + (u + 2), u)
                        gelu(i * 2 + (u + 1), (u + 1) % 2)
                gelu(BATCH - 1, 1)

            act.wait_ge(emb_link, 4 * BATCH)
            deviation(variances)
            with act.Fori(0, DEPTH) as l:
                act.wait_ge(fold_done, l + 1)
                attention(A, l)
                act.wait_ge(A.link, l * (A.tail * BATCH) + A.tail * BATCH)
                deviation(variances)
                act.wait_ge(wm_in, l * (16 * WM) + 16 * WM)
                mlp(l)
                act.wait_ge(m_link, l * (4 * BATCH) + 4 * BATCH)
                deviation(variances)
            act.wait_ge(n_link, 3 * BATCH)
            deviation(variances)
            attention(X, 0)
            act.wait_ge(X.link, X.tail * BATCH)
            deviation(variances)
            act.wait_ge(g_v, 1)
            deviation(s1[0:RT, :])

            def router_norm(n, u):
                act.wait_ge(r_t, n + 1)
                act.activation(yT[:, u, 0:NALL], misc[u][:, 0:NALL], ACT.Identity, bias=vec_f[:, 1:2],
                               scale=vec_f[:, 0:1]).then_inc(r_y, 1)

            with act.Fori(0, HALF) as i:
                for u in range(2):
                    router_norm(i * 2 + u, u)
            act.wait_ge(g_v, G_EXP)
            act.activation(top[0:RT, 3, :], top[0:RT, 2, :], ACT.Exp).then_inc(g_exp, 1)

            def expert_norm(n, u):
                act.wait_ge(e_t, n + 1)
                act.activation(yT[:, u, 0:NALL], misc[0][:, 0:NALL], ACT.Identity, bias=vec_y[:, 1:2],
                               scale=vec_y[:, 0:1]).then_inc(e_y, 1)

            def copy_gates(g, e):
                act.wait_ge(e_gb, g + 1)
                need(act, e_part, g - 1)
                act.activation(gates[:, e % 2, :], misc[1][:, 0:NALL], ACT.Copy).then_inc(e_gc, 1)

            def experts(n, u, first=False, last=False):
                for e in range(EXPERTS):
                    g = n * 8 + e
                    need(act, e_lo, g * 2 - 2)
                    for c in range(4):
                        act.wait_ge(e_f1, g * 4 + (c + 1))
                        act.activation(hid[:, e % 2, c, :], (plain + score)[c][:, 0:NALL], ACT.Gelu,
                                       bias=vec_f[:, 2 + 4 * e + c:3 + 4 * e + c], scale=1.0 / (XSCALE * WSCALE)).then_inc(e_g, 1)
                    if e >= LAG or not first:
                        copy_gates(g - LAG, e)
                    if e == 3 and not last:
                        expert_norm(n + 1, 1 - u)

            act.wait_ge(e_const, 2)
            act.wait_ge(split_p, PIECES)
            expert_norm(0, 0)
            experts(0, 0, first=True)
            experts(1, 1)
            with act.Fori(1, HALF - 1) as i:
                for u in range(2):
                    experts(i * 2 + u, u)
            experts(BATCH - 2, 0)
            experts(BATCH - 1, 1, last=True)
            for e in range(EXPERTS - LAG, EXPERTS):
                copy_gates((BATCH - 1) * 8 + e, e)

        @block.vector
        def _(dve):
            dve.memset(big[32:64, 0:2 * GRID * IMG], 0.0)
            dve.memset(wconv[32:64, :, :], 0.0)
            dve.memset(on[:, :], 0.0).then_inc(setup_v, 1)
            dve.memset(vaug[:, :, :, :, :], 1.0)
            dve.memset(negm[:, :, :, :], 0.0)
            dve.memset(mv[:, :], 1.0)
            dve.memset(eT[:, :, :], 0.0)
            dve.memset(rec[:, :, :], 0.0)
            dve.memset(bn[:, :, :, :], 0.0)
            for T in (A, X):
                for free in (*T.job_taken, T.out_ready):
                    dve.sem_inc(free, 1)
            dve.wait_ge(const_in, 16 * CONSTS)
            dve.tensor_copy(identb[:, :], ident[:, :])
            dve.tensor_copy(parts[:, :, :, :, :].rearrange("p a b c n -> p (a b c n)"), parts32).then_inc(parts_v, 1)
            dve.wait_ge(parts_v, 1)
            dve.memset(imgs[2][32:64, :], 0.0).then_inc(parts_v, 1)
            dve.tensor_copy(sel[:, :, :], sel32[:, :].unsqueeze(2).to_broadcast([P, HEADS, RT]))
            dve.tensor_tensor(posb[0:RT, :, :], on[0:RT, :].rearrange("p (t n) -> p t n", t=2),
                              probs[0:RT, 0, 0:2 * DIM].rearrange("p (t n) -> p t n", t=2),
                              ALU.add).then_inc(setup_v, 1)
            dve.wait_ge(setup_v, 2)
            dve.wait_ge(txt_in, 16)

            def stats_rows(b, tiles, link, v, slot=0):
                dve.wait_ge(link, v)
                dve.sem_inc(passed_v, 1)
                for t in tiles:
                    ins = dve.bn_stats(bn[0:ROWS[t], slot, t, :], h_tile(b, t))
                ins.then_inc(link, 1)

            def stats_joined(tiles, link, v, slot=0):
                dve.wait_ge(link, v)
                dve.sem_inc(passed_v, 1)
                for t in tiles:
                    ins = dve.bn_aggr(ag[0:ROWS[t], slot, t, :], bn[0:ROWS[t], slot, t, :])
                ins.then_inc(link, 1)

            def stats_kept(b, tiles, link, v, slot=0):
                dve.wait_ge(link, v)
                dve.sem_inc(passed_v, 1)
                if len(tiles) == 3:
                    dve.tensor_copy(mv[0:TXT, bass.ds(b * 6, 2)], ag[0:TXT, slot, 0, :])
                    tiles = tiles[1:]
                t0, rows = tiles[0], ROWS[tiles[0]]
                dve.tensor_copy(mv[0:rows, bass.ds(b * 6 + 2 * t0, 2 * len(tiles))],
                                ag[0:rows, slot, t0:t0 + len(tiles), :].rearrange("p t s -> p (t s)")).then_inc(link, 1)

            def stats(b, tiles, link, v):
                stats_rows(b, tiles, link, v)
                stats_joined(tiles, link, v + 1)
                stats_kept(b, tiles, link, v + 2)

            with dve.Fori(0, HALF) as i:
                for u in range(2):
                    b = i * 2 + u
                    dve.wait_ge(emb_done, b + 1)
                    dve.tensor_tensor(h_image(b), plain[u][0:RT, 0:2 * DIM],
                                      posb[0:RT, :, :].rearrange("p t n -> p (t n)"), ALU.add).then_inc(emb_link, 1)
                    stats(b, [0, 1, 2], emb_link, b * 4 + 1)

            def invert(count):
                dve.wait_ge(sd_ready, count)
                dve.reciprocal(rs[0:RT, :], sd[0:RT, :]).then_inc(rs_ready, 1)
                dve.wait_ge(rs_ready, count)

            def normalise(b, slot, tiles, scale):
                for k, t in enumerate(tiles):
                    ins = dve.tensor_scalar(xn[0:ROWS[t], slot, k, :], h_tile(b, t), mean(b, t), stat(scale, b, t),
                                            ALU.subtract, ALU.mult)
                return ins

            def take(T, s, base, name):
                bank, at = bank_of(T, name, s)
                dve.wait_ge(T.job_done[bank], base * T.phase_jobs + (at + 1))
                return misc[bank], T.job_taken[bank], base * T.phase_jobs + (at + 2)

            def norm_rows_of(T, s, base, wait):
                if wait:
                    bank, at = bank_of(T, "T", s.at(-2))
                    dve.wait_ge(T.job_done[bank], base * T.phase_jobs + (at + 1))
                normalise(s.sample, s.u % 2, [t[0] for t in T.tiles], rs).then_inc(T.xn_ready, 1)

            def high_part(T, s, base):
                _, _, count = take(T, s, base, "K")
                bank, _ = bank_of(T, "K", s)
                dve.wait_ge(T.job_taken[bank], count)
                dve.tensor_copy(hilo[:, s.u % 2, 0, :, 0:T.nq], qk[:, s.u % 2, :, 0:T.nq]).then_inc(T.hi_ready, 1)

            def take_queries(T, s, base, name):
                ps, taken, _ = take(T, s, base, name)
                block = ps[:, 0:T.cpj * T.nq].rearrange("p (c n) -> p c n", c=T.cpj)
                for half in range(2):
                    h0 = 2 * int(name[1]) * T.cpj + half
                    ins = dve.tensor_copy(qst[half * PART:(half + 1) * PART, s.u, h0:h0 + 2 * T.cpj - 1:2, 0:T.nq],
                                          block[half * PART:(half + 1) * PART, :, :])
                ins.then_inc(taken, 1)

            def max_unit(T, s, base, w):
                dve.wait_ge(T.plain_ready, (base * BATCH + s.n) * T.units + (w + 1))
                t = w // T.upt
                rows = T.tiles[t][1]
                h0 = (w % T.upt) * T.hpu
                src = plain[w % 2][0:rows, :].rearrange("p (j n) -> p j n", j=2)[:, :, 0:T.nk] if T.hpu == 2 \
                    else plain[w % 2][0:rows, 0:T.nk].unsqueeze(1)
                dve.tensor_reduce(negm[0:rows, s.u % 2, t, h0:h0 + T.hpu], src, AX.X, ALU.max,
                                  negate=True).then_inc(T.max_taken, 1)

            def end_image(T, s, base):
                ps, taken, _ = take(T, s, base, "E0")
                v = base * (T.tail * BATCH) + s.n * T.tail
                o = ps[0:RT, 0:512].rearrange("p (t h x) -> p t h x", t=2, h=HEADS)
                dve.reciprocal(rec[0:RT, :, :].unsqueeze(3), o[:, :, :, HD:HD + 1]).then_inc(T.link, 1)
                dve.wait_ge(T.link, v + 1)
                dve.tensor_tensor(on[0:RT, :].rearrange("p (t h d) -> p t h d", t=2, h=HEADS), o[:, :, :, 0:HD],
                                  rec[0:RT, :, :].unsqueeze(3).to_broadcast([RT, 2, HEADS, HD]),
                                  ALU.mult).then_inc(taken, 1)

            def end_projected(T, s, base):
                ps, taken, count = take(T, s, base, "E2")
                dve.wait_ge(T.bias_added, base * BATCH + s.n + 1)
                b = s.sample
                dve.tensor_tensor(h_image(b), ps[0:RT, 0:2 * DIM], h_image(b), ALU.add).then_inc(taken, 1)

            def end_stats(T, s, base, part):
                link, v = T.link, base * (T.tail * BATCH) + s.n * T.tail + T.tail - 3
                tiles = [t[0] for t in T.tiles]
                if part == 0:
                    if not T.cross:
                        bank, at = bank_of(T, "E2", s)
                        dve.wait_ge(T.job_taken[bank], base * T.phase_jobs + (at + 2))
                    stats_rows(s.sample, tiles, link, v)
                elif part == 1:
                    stats_joined(tiles, link, v + 1)
                else:
                    stats_kept(s.sample, tiles, link, v + 2)

            def end_cross(T, s, base, j):
                ps, taken, count = take(T, s, base, f"E{j}")
                v = s.n * T.tail + 2 * j
                t, rows, _, _ = T.tiles[j]
                o = ps[0:rows, 0:256].rearrange("p (h x) -> p h x", h=HEADS)
                dve.reciprocal(rec[0:rows, 0, :].unsqueeze(2), o[:, :, HD:HD + 1]).then_inc(T.link, 1)
                dve.wait_ge(T.link, v + 1)
                dve.tensor_tensor(on[0:rows, 0:DIM].rearrange("p (d h) -> p h d", h=HEADS), o[:, :, 0:HD],
                                  rec[0:rows, 0, :].unsqueeze(2).to_broadcast([rows, HEADS, HD]),
                                  ALU.mult).then_inc(taken, 1)
                dve.wait_ge(taken, count)
                b = s.sample
                dve.tensor_tensor(h_tile(b, t), h_tile(b, t), on[0:rows, 0:DIM], ALU.add).then_inc(T.link, 1)

            def attention(T, base):
                for m in range(LEAD):
                    norm_rows_of(T, Step(0, m), base, False)
                for m in range(LEAD):
                    high_part(T, Step(0, m), base)
                    for name in T.spread:
                        if name not in T.act_takes:
                            take_queries(T, Step(0, m), base, name)
                norm_rows_of(T, Step(0, LEAD), base, True)
                for w in range(T.units):
                    max_unit(T, Step(0, 0), base, w)

                def step(s):
                    inner = s.k is None
                    ahead = inner or s.k + LEAD < BATCH
                    more = inner or s.k + 1 < BATCH
                    for w in range(T.units):
                        if w == 1 and s.k != 0:
                            if T.cross:
                                end_cross(T, s.at(-1), base, 0)
                            else:
                                end_image(T, s.at(-1), base)
                        if w == 3:
                            if ahead:
                                high_part(T, s.at(LEAD), base)
                            if T.cross and s.k != 0:
                                end_cross(T, s.at(-1), base, 1)
                        if w == 5 and s.k != 0:
                            if T.cross:
                                end_cross(T, s.at(-1), base, 2)
                            else:
                                end_projected(T, s.at(-1), base)
                        if w == 6 and s.k != 0:
                            end_stats(T, s.at(-1), base, 0 if T.cross else 1)
                        if w == 7 and s.k != 0 and T.cross:
                            end_stats(T, s.at(-1), base, 2)
                        if w == (6 if T.cross else 2) and (inner or s.k + LEAD + 1 < BATCH):
                            norm_rows_of(T, s.at(LEAD + 1), base, True)
                        if w == 6 and s.k != 0 and T.cross:
                            end_stats(T, s.at(-1), base, 1)
                        if ahead and T.cross:
                            for name in T.spread_at.get(w, ()):
                                if name not in T.act_takes:
                                    take_queries(T, s.at(LEAD), base, name)
                        if more:
                            for x in T.plain_at(s, w):
                                max_unit(T, s.at(1), base, x)
                        if not T.cross and s.k != 0 and w in (5, 7):
                            end_stats(T, s.at(-1), base, 0 if w == 5 else 2)
                    if not T.cross and ahead:
                        take_queries(T, s.at(LEAD), base, "q1")

                for u in range(SLOTS):
                    step(Step(0, u))
                with dve.Fori(0, (BATCH // SLOTS - 2) // 2) as i:
                    for u in range(2 * SLOTS):
                        step(Step(i * 2 + 1, u))
                for u in range(SLOTS):
                    step(Step(BATCH // SLOTS - 1, u))
                last = Step(BATCH // SLOTS - 1, SLOTS - 1)
                if T.cross:
                    for j in range(3):
                        end_cross(T, last, base, j)
                else:
                    end_image(T, last, base)
                    end_projected(T, last, base)
                for part in range(3):
                    end_stats(T, last, base, part)

            def mlp(l):
                def norm(n, u, wait=True):
                    if wait:
                        dve.wait_ge(m_t, l * BATCH + n - 1)
                    normalise(n, u, [1, 2], rs).then_inc(m_xn, 1)

                def residual(n, u):
                    dve.wait_ge(m_f2, l * BATCH + n + 1)
                    dve.wait_ge(m_bias, l * BATCH + n + 1)
                    dve.tensor_tensor(h_image(n), score[u][0:RT, 0:2 * DIM], h_image(n), ALU.add).then_inc(m_link, 1)

                def pair(a, ahead=2):
                    b, v, tiles = a + 1, (l * BATCH + a) * 4, [1, 2]
                    if ahead:
                        norm(a + 3, 1)
                    residual(a, 0)
                    if ahead == 2:
                        norm(a + 4, 0)
                    stats_rows(a, tiles, m_link, v + 1)
                    residual(b, 1)
                    stats_joined(tiles, m_link, v + 2)
                    stats_rows(b, tiles, m_link, v + 3, 1)
                    stats_kept(a, tiles, m_link, v + 4)
                    stats_joined(tiles, m_link, v + 5, 1)
                    stats_kept(b, tiles, m_link, v + 7, 1)

                norm(0, 0, False)
                norm(1, 1, False)
                norm(2, 0)
                with dve.Fori(0, (HALF - 2) // PAIRS_PER_PASS) as i:
                    for k in range(PAIRS_PER_PASS):
                        pair(i * (2 * PAIRS_PER_PASS) + 2 * k)
                pair(BATCH - 4, 1)
                pair(BATCH - 2, 0)

            dve.wait_ge(emb_link, 4 * BATCH)
            dve.memset(qst_words, 0.0)
            with dve.Fori(0, DEPTH) as l:
                dve.wait_ge(wa_in, l * (16 * WA) + 16 * WA)
                dve.tensor_scalar(row_v[:, :], ident[:, :], 0.0, vec_a[:, 4:5], ALU.mult, ALU.add)
                dve.tensor_scalar(qbias[:, :], vec_a[:, 2:3], float(HD) ** -0.5, None, ALU.mult).then_inc(fold_v, 1)
                dve.wait_ge(fold_pe, l + 1)
                dve.tensor_tensor(row_a[0:RT, :], plain[0][0:RT, 0:DIM], row_a[0:RT, :], ALU.add).then_inc(fold_done, 1)
                invert(l * 2 + 1)
                attention(A, l)
                invert(l * 2 + 2)
                mlp(l)
            invert(2 * DEPTH + 1)

            def final_norm(n):
                for t in (1, 2):
                    ins = dve.tensor_scalar(h_tile(n, t), h_tile(n, t), mean(n, t), stat(rs, n, t),
                                            ALU.subtract, ALU.mult)
                ins.then_inc(n_xn, 1)

            def final_stats(a):
                v, tiles = a * 3, [1, 2]
                for k in range(2):
                    dve.wait_ge(n_h, a + (k + 1))
                    if k:
                        stats_rows(a + 1, tiles, n_link, v + 1, 1)
                    else:
                        dve.sem_inc(passed_v, 1)
                        for t in tiles:
                            ins = dve.bn_stats(bn[0:RT, 0, t, :], h_tile(a, t))
                        ins.then_inc(n_link, 1)
                for k in range(2):
                    stats_joined(tiles, n_link, v + k + 1, k)
                for k in range(2):
                    stats_kept(a + k, tiles, n_link, v + k + 3, k)

            final_norm(0)
            final_norm(1)
            def final_pair(a):
                final_norm(a + 2)
                final_norm(a + 3)
                final_stats(a)

            with dve.Fori(0, (HALF - 2) // PAIRS_PER_PASS) as i:
                for k in range(PAIRS_PER_PASS):
                    final_pair(i * (2 * PAIRS_PER_PASS) + 2 * k)
            final_pair(BATCH - 4)
            final_stats(BATCH - 2)
            invert(2 * DEPTH + 2)
            attention(X, 0)
            invert(2 * DEPTH + 3)

            count = [0]

            def link(ins):
                count[0] += 1
                ins.then_inc(g_v, 1)
                dve.wait_ge(g_v, count[0])

            r, r2 = rs[0:RT, :], rr[0:RT, :]
            pairs = mv[0:RT, :].rearrange("p (n s) -> p n s", s=2)
            dve.tensor_tensor(s2[0:RT, :], pairs[:, :, 1], r, ALU.mult).then_inc(fold_v, 1)
            dve.wait_ge(fold_v, DEPTH + 1)
            link(dve.tensor_tensor(s1[0:RT, :], s2[0:RT, :], r, ALU.mult))
            dve.wait_ge(sd_ready, 2 * DEPTH + 4)
            link(dve.reciprocal(s2[0:RT, :], sd[0:RT, :]))
            link(dve.tensor_tensor(r2, s2[0:RT, :], r, ALU.mult))
            link(dve.tensor_scalar(s1[0:RT, :], r, 1.0, None, ALU.add))
            link(dve.tensor_tensor(s2[0:RT, :], pairs[:, :, 0], r, ALU.mult))
            link(dve.memset(logit[:, :], 0.0))

            def router_rows(n, u, wait=True):
                if wait:
                    dve.wait_ge(r_t, n - 1)
                normalise(n, u, range(3), rr).then_inc(r_xn, 1)

            def router_logits(n, u):
                dve.wait_ge(r_l, n + 1)
                for lo, k, rows in ((0, 1, TXT), (1, 2, RT)):
                    ins = dve.tensor_tensor(
                        logit[0:rows, bass.ds(n * 24 + lo * EXPERTS, k * EXPERTS)],
                        plain[u][0:rows, lo * EXPERTS:(lo + k) * EXPERTS], br2[0:rows, 0:k * EXPERTS], ALU.add)
                ins.then_inc(r_done, 1)

            for k in range(2):
                ins = dve.tensor_copy(br2[0:RT, k * EXPERTS:(k + 1) * EXPERTS], b_r[0:RT, :])
            link(ins)
            router_rows(0, 0, False)
            router_rows(1, 1, False)
            router_rows(2, 0)
            router_logits(0, 0)
            with dve.Fori(0, (HALF - 2) // PAIRS_PER_PASS) as i:
                for k in range(2 * PAIRS_PER_PASS):
                    n = i * (2 * PAIRS_PER_PASS) + (k + 1)
                    router_rows(n + 2, (k + 1) % 2)
                    router_logits(n, (k + 1) % 2)
            router_rows(BATCH - 1, 1)
            for n in range(BATCH - 3, BATCH):
                router_logits(n, n % 2)
            dve.wait_ge(r_done, BATCH)

            n3 = BATCH * 3
            cube = lambda a: a[0:RT, :].rearrange("p (n e) -> p n e", e=EXPERTS)
            wide = lambda k: top[0:RT, k, :].unsqueeze(2).to_broadcast([RT, n3, EXPERTS])
            ranks = rank[0:RT, :].unsqueeze(1).to_broadcast([RT, n3, EXPERTS])
            L, G, TA, TB = cube(logit), cube(gate), cube(ga), cube(gb)

            def pick(src, best, first, chosen):
                link(dve.tensor_reduce(top[0:RT, best, :], src, AX.X, ALU.max))
                link(dve.tensor_tensor(chosen, src, wide(best), ALU.is_equal))
                link(dve.tensor_tensor(chosen, chosen, ranks, ALU.mult))
                link(dve.tensor_reduce(top[0:RT, first, :], chosen, AX.X, ALU.max))
                link(dve.tensor_tensor(chosen, chosen, wide(first), ALU.is_equal))

            pick(L, 0, 4, TA)
            link(dve.scalar_tensor_tensor(out=L, in0=TA, scalar=-3.0e38, in1=L, op0=ALU.mult, op1=ALU.add))
            pick(L, 1, 5, TB)
            link(dve.tensor_tensor(top[0:RT, 2, :], top[0:RT, 1, :], top[0:RT, 0, :], ALU.subtract))
            assert count[0] == G_EXP
            dve.wait_ge(g_exp, 1)
            link(dve.tensor_scalar(top[0:RT, 4, :], top[0:RT, 3, :], 1.0, None, ALU.add))
            link(dve.reciprocal(top[0:RT, 0, :], top[0:RT, 4, :]))
            link(dve.tensor_tensor(top[0:RT, 1, :], top[0:RT, 3, :], top[0:RT, 0, :], ALU.mult))
            link(dve.tensor_tensor(TA, TA, wide(0), ALU.mult))
            link(dve.tensor_tensor(TB, TB, wide(1), ALU.mult))
            link(dve.tensor_tensor(G, TA, TB, ALU.add))
            assert count[0] == G_ALL

            def expert_rows(n, u):
                need(dve, e_t, n - 1)
                normalise(n, u, range(3), rr).then_inc(e_xn, 1)

            def expert_gates(n):
                need(dve, e_gt, n)
                dve.sem_inc(passed_v, 1)
                now = gate[0:RT, bass.ds(n * 24, 24)].rearrange("p (t e) -> p t e", t=3)
                dve.tensor_copy(gnow[0:RT, :, 0:EXPERTS], now)
                dve.tensor_copy(gnow[0:RT, :, GROUP:GROUP + EXPERTS], now).then_inc(e_gn, 1)

            def take_gates(n, u):
                low = slice(GROUP, GROUP + EXPERTS)
                dve.wait_ge(e_gt, n + 1)
                dve.tensor_copy(gate16[0:GROUP + EXPERTS, u, 0:NALL],
                                misc[0][0:GROUP + EXPERTS, 0:NALL]).then_inc(e_gs, 1)
                dve.tensor_copy(gateT[:, u, 0:NALL], misc[0][0:EXPERTS, 0:NALL]).then_inc(e_gs, 1)
                dve.wait_ge(e_gs, n * 3 + 1)
                dve.tensor_tensor(gate16[low, u, 0:NALL], misc[0][low, 0:NALL], gate16[low, u, 0:NALL],
                                  ALU.subtract).then_inc(e_gs, 1)

            def take_bias(n, u):
                dve.wait_ge(e_b2, n + 1)
                dve.tensor_copy(acc[:, u, :], misc[0][:, 0:NALL]).then_inc(e_b2t, 1)

            def high_input(n, u):
                dve.wait_ge(e_y, n + 1)
                dve.tensor_copy(y16[:, u, 0, 0:NALL], yT[:, u, 0:NALL]).then_inc(e_yhi, 1)

            def add_expert(n, u, e):
                g = n * 8 + e
                dve.wait_ge(e_gc, g + 1)
                dve.wait_ge(e_f2, g + 1)
                if e == 0:
                    dve.wait_ge(e_b2t, n + 1)
                need(dve, e_acc, g)
                dve.scalar_tensor_tensor(out=part_out, in0=outp[e % 2][:, 0:NALL], scalar=1.0 / WSCALE,
                                         in1=gates[:, e % 2, :], op0=ALU.mult, op1=ALU.mult).then_inc(e_part, 1)
                dve.wait_ge(e_part, g + 1)
                dve.tensor_tensor(acc[:, u, :], acc[:, u, :], part_out, ALU.add).then_inc(e_acc, 1)

            def scale_rows(n):
                for t in range(3):
                    ins = dve.tensor_scalar(h_tile(n, t), h_tile(n, t), stat(s1, n, t), stat(s2, n, t),
                                            ALU.mult, ALU.subtract)
                ins.then_inc(e_s, 1)

            def complete_rows(n):
                dve.wait_ge(e_s, n + 1)
                dve.wait_ge(e_back, n + 1)
                dve.tensor_tensor(h_tile(n, 0), misc[0][0:TXT, 0:DIM], h_tile(n, 0), ALU.add)
                dve.tensor_tensor(h_image(n), misc[0][0:RT, DIM:3 * DIM], h_image(n), ALU.add).then_inc(e_h, 1)

            def experts(n, u, first=False, last=False):
                for e in range(EXPERTS):
                    for k in range(0, 4, 2):
                        dve.wait_ge(e_g, (n * 8 + e) * 4 + (k + 2))
                        dve.tensor_copy(hid16[e % 4][:, 0, k:k + 2, :], hid[:, e % 2, k:k + 2, :]).then_inc(e_hi, 1)
                    if e >= LAG:
                        add_expert(n, u, e - LAG)
                    elif not first:
                        add_expert(n - 1, 1 - u, e - LAG + EXPERTS)
                    if e == 1 and not last:
                        expert_gates(n + 1)
                    if e == 0 and not last:
                        expert_rows(n + 1, 1 - u)
                    if e == 2 and not first:
                        complete_rows(n - 1)
                    if e == 3:
                        scale_rows(n)
                    if e == 5 and not last:
                        high_input(n + 1, 1 - u)
                    if e == 5 and not last:
                        take_gates(n + 1, 1 - u)
                    if e == 7 and not last:
                        take_bias(n + 1, 1 - u)

            dve.tensor_copy(gsel, sel32_e[:, :].unsqueeze(2).to_broadcast([P, EXPERTS, P]))
            dve.memset(gnow, 0.0)
            dve.memset(gate16, 0.0).then_inc(e_const, 1)
            dve.tensor_scalar(vec_y[:, :], vec_f[:, 0:2], XSCALE, None, ALU.mult).then_inc(e_const, 1)
            dve.wait_ge(e_const, 2)
            dve.wait_ge(split_p, PIECES)
            expert_rows(0, 0)
            expert_gates(0)
            high_input(0, 0)
            take_gates(0, 0)
            take_bias(0, 0)
            experts(0, 0, first=True)
            experts(1, 1)
            with dve.Fori(1, HALF - 1) as i:
                for u in range(2):
                    experts(i * 2 + u, u)
            experts(BATCH - 2, 0)
            experts(BATCH - 1, 1, last=True)
            for e in range(EXPERTS - LAG, EXPERTS):
                add_expert(BATCH - 1, 1, e)
            complete_rows(BATCH - 1)

        @block.gpsimd
        def _(pool):
            pool.wait_ge(const_in, 16 * CONSTS)

            def low_part(T, s, base):
                pool.wait_ge(T.hi_ready, base * BATCH + s.n + 1)
                pool.tensor_tensor(hilo[:, s.u % 2, 1, :, 0:T.nq], qk[:, s.u % 2, :, 0:T.nq],
                                   hilo[:, s.u % 2, 0, :, 0:T.nq], ALU.subtract).then_inc(T.lo_ready, 1)

            def add_bias(b, row):
                pool.sem_inc(passed_p, 1)
                image = h_image(b).rearrange("p (t n) -> p t n", t=2)
                return pool.tensor_tensor(image, image, row.unsqueeze(1).to_broadcast([RT, 2, DIM]), ALU.add)

            def add_output_bias(T, s, base):
                if T.cross:
                    return
                pool.wait_ge(T.xn_ready, base * BATCH + s.n + 1)
                add_bias(s.sample, row_a[0:RT, :]).then_inc(T.bias_added, 1)

            def attention(T, base):
                for m in range(LEAD):
                    low_part(T, Step(0, m), base)
                    add_output_bias(T, Step(0, m), base)

                def step(s):
                    if s.k is None or s.k + LEAD < BATCH:
                        low_part(T, s.at(LEAD), base)
                        add_output_bias(T, s.at(LEAD), base)

                for u in range(SLOTS):
                    step(Step(0, u))
                with pool.Fori(0, (BATCH // SLOTS - 2) // 2) as i:
                    for u in range(2 * SLOTS):
                        step(Step(i * 2 + 1, u))
                for u in range(SLOTS):
                    step(Step(BATCH // SLOTS - 1, u))

            with pool.Fori(0, DEPTH) as l:
                pool.wait_ge(fold_done, l + 1)
                attention(A, l)
                pool.wait_ge(wm_in, l * (16 * WM) + 16 * WM)
                pool.sem_inc(passed_p, 1)
                with pool.Fori(0, BATCH) as b:
                    pool.wait_ge(m_xn, l * BATCH + b + 1)
                    add_bias(b, row_m[0:RT, :]).then_inc(m_bias, 1)
            def final_affine(b):
                pool.wait_ge(n_xn, b + 1)
                pool.sem_inc(passed_p, 1)
                image = h_image(b).rearrange("p (t n) -> p t n", t=2)
                wide = [RT, 2, DIM]
                pool.tensor_tensor(image, image, norm_rows[0:RT, 0, :].unsqueeze(1).to_broadcast(wide),
                                   ALU.mult).then_inc(n_w, 1)
                pool.wait_ge(n_w, b + 1)
                pool.sem_inc(passed_p, 1)
                pool.tensor_tensor(image, image, norm_rows[0:RT, 1, :].unsqueeze(1).to_broadcast(wide),
                                   ALU.add).then_inc(n_h, 1)

            with pool.Fori(0, HALF // 2) as i:
                for k in range(4):
                    final_affine(i * 4 + k)
            attention(X, 0)
            for w in range(PIECES):
                pool.wait_ge(moe_in[w % STAGES], 16 * (w // STAGES + 1))
                piece, hi, lo = stage[:, w % STAGES, :, :], wparts[:, w, 0, :, :], wparts[:, w, 1, :, :]
                pool.tensor_scalar(piece, piece, WSCALE, None, ALU.mult).then_inc(split_hi, 1)
                pool.wait_ge(split_hi, w * 2 + 1)
                pool.tensor_copy(hi, piece).then_inc(split_hi, 1)
                pool.wait_ge(split_hi, w * 2 + 2)
                pool.tensor_tensor(lo, piece, hi, ALU.subtract).then_inc(split_p, 1)

            def low_input(n, u):
                pool.wait_ge(e_yhi, n + 1)
                pool.tensor_tensor(y16[:, u, 1, 0:NALL], yT[:, u, 0:NALL], y16[:, u, 0, 0:NALL],
                                   ALU.subtract).then_inc(e_ylo, 1)

            def experts(n, u, last=False):
                for e in range(EXPERTS):
                    for k in range(0, 4, 2):
                        pool.wait_ge(e_hi, (n * 8 + e) * 2 + (k // 2 + 1))
                        pool.tensor_tensor(hid16[e % 4][:, 1, k:k + 2, :], hid[:, e % 2, k:k + 2, :],
                                           hid16[e % 4][:, 0, k:k + 2, :], ALU.subtract).then_inc(e_lo, 1)
                    if e == 5 and not last:
                        low_input(n + 1, 1 - u)

            low_input(0, 0)
            experts(0, 0)
            experts(1, 1)
            with pool.Fori(1, HALF - 1) as i:
                for u in range(2):
                    experts(i * 2 + u, u)
            experts(BATCH - 2, 0)
            experts(BATCH - 1, 1, last=True)


def kernel(**inputs):
    import numpy as np
    import concourse.bacc as bacc
    from concourse.bass_utils import run_bass_kernel_spmd as run

    a = {k: np.asarray(v) for k, v in inputs.items()}
    t = {k[len("L0_tok_"):]: v for k, v in a.items() if k.startswith("L0_tok_")}
    f = {k[len("L0_ffn_"):]: v for k, v in a.items() if k.startswith("L0_ffn_")}
    cols = [t["ln1_w"], t["ln1_b"]] + [t["qkv_b"][:, k * DIM:(k + 1) * DIM] for k in range(3)]
    cols += [t["ln2_w"], t["ln2_b"], t["fc1_b"][:, 0:DIM], t["fc1_b"][:, DIM:HID]]
    conv = t["conv_w"].reshape(CROWS, 2, PIX, DIM).transpose(1, 0, 2, 3)
    row = np.arange(P)
    feature = (row // PART) * HD + row % HD
    piece = row % PART // HD
    parts = np.zeros((P, 2, 2, PAIRS, P), np.float32)
    for side, wanted in enumerate((piece % 2, piece // 2)):
        for part in range(2):
            for pair in range(PAIRS):
                parts[pair * 2 * HD + feature, side, part, pair, row] = wanted == part
    laid = {
        "x": a["x"].reshape(BATCH * 3, GRID, PATCH, IMG).transpose(0, 2, 1, 3),
        "txt": a["txt"],
        "conv_w": conv,
        "conv_b": t["conv_b"],
        "cls": t["cls_token"].reshape(1, DIM),
        "pos": t["pos_embed"].reshape(NTOK, DIM),
        "qkv_w": t["qkv_w"],
        "proj_w": t["proj_w"],
        "fc1_w": t["fc1_w"],
        "fc2_w": t["fc2_w"],
        "vec": np.stack(cols, axis=2),
        "rows": np.stack([t["proj_b"], t["fc2_b"]], axis=1).reshape(2 * DEPTH, DIM),
        "norm": np.stack([t["norm_w"], t["norm_b"]]),
        "x_w": np.concatenate([a["L0_attn_q_w"], a["L0_attn_kv_w"]]).T,
        "vec_f": np.concatenate([f["ln_g"][:, None], f["ln_b"][:, None],
                                 f["b1"].reshape(EXPERTS * 4, DIM).T], axis=1),
        "w_r": f["w_r"].T,
        "b_r": f["b_r"],
        "w1": f["W1"],
        "w2": f["W2"],
        "b2": f["b2"],
        "c_ident": np.eye(P, dtype=np.float32),
        "c_parts": parts.reshape(P, 16 * P),
        "c_sel": (np.arange(P)[:, None] == np.arange(HEADS)[None]).astype(np.float32),
        "c_sel_e": (np.arange(P)[:, None] % GROUP == np.arange(EXPERTS)[None]).astype(np.float32)
        * (np.arange(P) < GROUP + EXPERTS)[:, None],
        "c_rank": np.arange(EXPERTS, 0, -1).astype(np.float32),
        "c_eps": np.full((P, 1), EPS, np.float32),
    }
    nc = bacc.Bacc("TRN2", target_bir_lowering=False, num_devices=1)
    arrays, args = {}, {}
    for name, array in laid.items():
        array = np.ascontiguousarray(array)
        arrays[f"in_{name}"] = array
        args[name] = nc.dram_tensor(f"in_{name}", array.shape, mybir.dt.from_np(array.dtype), kind="ExternalInput").ap()
    out = nc.dram_tensor("out_0", (BATCH, NTOK + TXT, DIM), F32, kind="ExternalOutput").ap()
    fusion_kernel(nc, args, out)
    result = run(nc, [arrays], core_ids=[0])
    return result.results[0]["out_0"]
```
